# Optimizing a Trainium2 kernel written in Bass

```python
import numpy as np
import jax
import jax.numpy as jnp

def _softmax(x, axis=-1):
    return jax.nn.softmax(x, axis=axis)

def _gelu(x):
    return jax.nn.gelu(x, approximate=True)

def _silu(x):
    return jax.nn.silu(x)

def _sigmoid(x):
    return jax.nn.sigmoid(x)

def _layernorm(x, axis=-1, eps=1e-05):
    m = jnp.mean(x, axis=axis, keepdims=True)
    v = jnp.var(x, axis=axis, keepdims=True)
    return (x - m) / jnp.sqrt(v + eps)

def _scatter_add(tgt, idx, src, axis=0):
    return tgt.at[idx].add(src)

def _segment_sum(src, seg, n):
    return jax.ops.segment_sum(src, seg, n)
kernel_name = 'mk_adj_preln_d2_adj_r2_c37f3e'

def setup_inputs(seed: int=0):
    np.random.seed(seed)
    _w = jnp.asarray

    def _rec_inputs():
        import jax
        import jax.numpy as jnp
        _gk = jax.random.key(seed)
        x = -0.000125 + 0.9999 * jax.random.normal(jax.random.fold_in(_gk, 1), (64, 128, 128), jnp.float32)
        _a = jax.random.bernoulli(jax.random.fold_in(_gk, 2), 0.03125, (128, 128))
        _a = jnp.logical_or(_a, jnp.swapaxes(_a, -1, -2))
        _a = jnp.logical_or(_a, jnp.eye(128, dtype=bool))
        _af = _a.astype(jnp.float32)
        _af = _af * jax.random.uniform(jax.random.fold_in(_gk, 3), (128, 128), jnp.float32, 0.05, 0.000488281)
        adj = _af
        return (x, adj)
    x, adj = _rec_inputs()

    def _L0_gnn_setup():
        import jax, jax.numpy as jnp
        import numpy as np
        B, T, D, H = (64, 1024, 128, 128)
        MAX_SKIP = 4

        def _lstm_last(Wih, Whh, bih, bhh, xs):
            N, _, Hd = xs.shape
            bias = bih + bhh

            def step(carry, x_t):
                h, c = carry
                g = x_t @ Wih.T + h @ Whh.T + bias
                i, f, gg, o = jnp.split(g, 4, axis=-1)
                c = jax.nn.sigmoid(f) * c + jax.nn.sigmoid(i) * jnp.tanh(gg)
                h = jax.nn.sigmoid(o) * jnp.tanh(c)
                return ((h, c), None)
            init = (jnp.zeros((N, Hd), xs.dtype), jnp.zeros((N, Hd), xs.dtype))
            (h_last, _), _ = jax.lax.scan(step, init, jnp.swapaxes(xs, 0, 1))
            return h_last
        key = jax.random.key(seed)
        ks = jax.random.split(key, 8)
        s = 0.05
        x = jax.random.normal(ks[0], (B, T, D), jnp.float32)
        adj = jax.random.uniform(ks[1], (T, T), jnp.float32) / T
        Wg0 = jax.random.normal(ks[2], (D, H), jnp.float32) * s
        bg0 = jnp.zeros((H,), jnp.float32)
        Wg1 = jax.random.normal(ks[3], (H, H), jnp.float32) * s
        bg1 = jnp.zeros((H,), jnp.float32)
        Wih = jax.random.normal(ks[4], (MAX_SKIP, 4 * H, H), jnp.float32) * s
        Whh = jax.random.normal(ks[5], (MAX_SKIP, 4 * H, H), jnp.float32) * s
        bih = jax.random.normal(ks[6], (MAX_SKIP, 4 * H), jnp.float32) * s
        bhh = jax.random.normal(ks[7], (MAX_SKIP, 4 * H), jnp.float32) * s
        return dict(x=x, adj=adj, Wg0=Wg0, bg0=bg0, Wg1=Wg1, bg1=bg1, Wih=Wih, Whh=Whh, bih=bih, bhh=bhh)
    _L0_gnn_all = _L0_gnn_setup()
    _L0_gnn_in = {k: v for k, v in _L0_gnn_all.items() if k in ('Wg0', 'bg0', 'Wg1', 'bg1', 'Wih', 'Whh', 'bih', 'bhh')}
    del _L0_gnn_all

    def _L1_gnn_setup():
        import jax, jax.numpy as jnp
        import numpy as np
        EPS = 1e-05

        def _batchnorm(x, gamma, beta):
            mu = jnp.mean(x, axis=0)
            var = jnp.var(x, axis=0)
            return (x - mu) * jax.lax.rsqrt(var + EPS) * gamma + beta
        key = jax.random.key(seed)
        ks = jax.random.split(key, 4)
        b, n, d, h, o = (32, 1024, 128, 256, 128)
        features = jax.random.normal(ks[0], (b, n, d), dtype=jnp.float32)
        A = jax.random.uniform(ks[1], (n, n), dtype=jnp.float32)
        lim1 = float(np.sqrt(6.0 / (d + h)))
        W1 = jax.random.uniform(ks[2], (h, d), minval=-lim1, maxval=lim1, dtype=jnp.float32)
        b1 = jnp.zeros((h,), jnp.float32)
        lim2 = float(np.sqrt(6.0 / (h + o)))
        W2 = jax.random.uniform(ks[3], (o, h), minval=-lim2, maxval=lim2, dtype=jnp.float32)
        b2 = jnp.zeros((o,), jnp.float32)
        g1 = jnp.ones((h,), jnp.float32)
        be1 = jnp.zeros((h,), jnp.float32)
        g2 = jnp.ones((o,), jnp.float32)
        be2 = jnp.zeros((o,), jnp.float32)
        return {'features': features, 'A': A, 'W1': W1, 'b1': b1, 'g1': g1, 'be1': be1, 'W2': W2, 'b2': b2, 'g2': g2, 'be2': be2}
    _L1_gnn_all = _L1_gnn_setup()
    _L1_gnn_in = {k: v for k, v in _L1_gnn_all.items() if k in ('W1', 'b1', 'g1', 'be1', 'W2', 'b2', 'g2', 'be2')}
    del _L1_gnn_all
    return {'x': x, 'adj': adj, 'L0_gnn_Wg0': _L0_gnn_in['Wg0'], 'L0_gnn_bg0': _L0_gnn_in['bg0'], 'L0_gnn_Wg1': _L0_gnn_in['Wg1'], 'L0_gnn_bg1': _L0_gnn_in['bg1'], 'L0_gnn_Wih': _L0_gnn_in['Wih'], 'L0_gnn_Whh': _L0_gnn_in['Whh'], 'L0_gnn_bih': _L0_gnn_in['bih'], 'L0_gnn_bhh': _L0_gnn_in['bhh'], 'L1_gnn_W1': _L1_gnn_in['W1'], 'L1_gnn_b1': _L1_gnn_in['b1'], 'L1_gnn_g1': _L1_gnn_in['g1'], 'L1_gnn_be1': _L1_gnn_in['be1'], 'L1_gnn_W2': _L1_gnn_in['W2'], 'L1_gnn_b2': _L1_gnn_in['b2'], 'L1_gnn_g2': _L1_gnn_in['g2'], 'L1_gnn_be2': _L1_gnn_in['be2']}

def reference(x, adj, L0_gnn_Wg0, L0_gnn_bg0, L0_gnn_Wg1, L0_gnn_bg1, L0_gnn_Wih, L0_gnn_Whh, L0_gnn_bih, L0_gnn_bhh, L1_gnn_W1, L1_gnn_b1, L1_gnn_g1, L1_gnn_be1, L1_gnn_W2, L1_gnn_b2, L1_gnn_g2, L1_gnn_be2):
    import jax
    import jax.numpy as jnp

    def _L0_gnn_ref(x, adj, Wg0, bg0, Wg1, bg1, Wih, Whh, bih, bhh):
        import jax, jax.numpy as jnp
        import numpy as np
        B, T, D, H = (64, 1024, 128, 128)
        MAX_SKIP = 4

        def _lstm_last(Wih, Whh, bih, bhh, xs):
            N, _, Hd = xs.shape
            bias = bih + bhh

            def step(carry, x_t):
                h, c = carry
                g = x_t @ Wih.T + h @ Whh.T + bias
                i, f, gg, o = jnp.split(g, 4, axis=-1)
                c = jax.nn.sigmoid(f) * c + jax.nn.sigmoid(i) * jnp.tanh(gg)
                h = jax.nn.sigmoid(o) * jnp.tanh(c)
                return ((h, c), None)
            init = (jnp.zeros((N, Hd), xs.dtype), jnp.zeros((N, Hd), xs.dtype))
            (h_last, _), _ = jax.lax.scan(step, init, jnp.swapaxes(xs, 0, 1))
            return h_last
        h = jax.nn.relu(jnp.einsum('ts,bsh->bth', adj, x @ Wg0 + bg0))
        h = jax.nn.relu(jnp.einsum('ts,bsh->bth', adj, h @ Wg1 + bg1))
        Bv, Tv, Hd = h.shape
        for p in range(1, MAX_SKIP + 1):
            nw = Tv // p
            wins = h[:, :nw * p, :].reshape(Bv * nw, p, Hd)
            last = _lstm_last(Wih[p - 1], Whh[p - 1], bih[p - 1], bhh[p - 1], wins)
            idx = jnp.arange(nw) * p + (p - 1)
            h = h.at[:, idx, :].set(last.reshape(Bv, nw, Hd))
        return h

    def _L1_gnn_ref(features, A, W1, b1, g1, be1, W2, b2, g2, be2):
        import jax, jax.numpy as jnp
        import numpy as np
        EPS = 1e-05

        def _batchnorm(x, gamma, beta):
            mu = jnp.mean(x, axis=0)
            var = jnp.var(x, axis=0)
            return (x - mu) * jax.lax.rsqrt(var + EPS) * gamma + beta
        b, n, d = features.shape
        A_norm = A + jnp.eye(n, dtype=A.dtype)
        deg = jnp.sum(A_norm, axis=0) + jnp.sum(A_norm, axis=1) - jnp.diagonal(A_norm)
        dinv = jax.lax.rsqrt(deg)
        A_hat = A_norm * dinv[:, None] * dinv[None, :]
        agg = jnp.einsum('nm,bmd->bnd', A_hat, features)
        x = agg.reshape(-1, d)
        h = jax.nn.relu(_batchnorm(x @ W1.T + b1, g1, be1))
        out = h @ W2.T + b2
        out = _batchnorm(out, g2, be2)
        return out.reshape(b, n, -1)
    h = jnp.maximum(_layernorm(x, axis=-1), 0.0)
    x = x + _L0_gnn_ref(h, adj, L0_gnn_Wg0, L0_gnn_bg0, L0_gnn_Wg1, L0_gnn_bg1, L0_gnn_Wih, L0_gnn_Whh, L0_gnn_bih, L0_gnn_bhh)
    h = jnp.maximum(_layernorm(x, axis=-1), 0.0)
    x = x + _L1_gnn_ref(h, adj, L1_gnn_W1, L1_gnn_b1, L1_gnn_g1, L1_gnn_be1, L1_gnn_W2, L1_gnn_b2, L1_gnn_g2, L1_gnn_be2)
    return x

_drawn_inputs = setup_inputs


def setup_inputs(seed=0):
    import zlib

    import numpy as np

    out = dict(_drawn_inputs(seed))
    spreads = {'L0_gnn_bg0': (0.0, 0.8),
     'L0_gnn_bg1': (0.0, 0.8),
     'L1_gnn_b1': (0.0, 0.8),
     'L1_gnn_g1': (1.0, 0.2),
     'L1_gnn_be1': (0.0, 0.1),
     'L1_gnn_b2': (0.0, 0.8),
     'L1_gnn_g2': (1.0, 0.2),
     'L1_gnn_be2': (0.0, 0.1)}
    factors = {'L0_gnn_Wg0': 8.0, 'L0_gnn_Wg1': 8.0, 'L0_gnn_Wih': 8.0, 'L0_gnn_Whh': 8.0}
    for name, (base, spread) in spreads.items():
        noise = np.random.default_rng([zlib.crc32(name.encode()), seed]).standard_normal(out[name].shape)
        drawn = base * np.exp(spread * noise) if base else spread * noise
        out[name] = jnp.asarray(drawn.astype(out[name].dtype))
    for name, factor in factors.items():
        out[name] = (out[name] * factor).astype(out[name].dtype)
    return out
```

```python
import concourse.bass as bass
from concourse import mybir
from contextlib import ExitStack

P = 128
NB = 64
TB = 4
NT = NB // TB
TC = TB * P
GB = 8
NG = NB // GB
SKIPS = 4
EPS = 1e-5
I_, F_, G_, O_ = range(4)
H1 = 2


def at_least(engine, sem, value):
    if isinstance(value, int) and value < 1:
        return
    engine.wait_ge(sem, value)


def gnn_kernel(nc, x, adj, adjT, gcn_w, gcn_b, lstm_w, lstm_b, lin1_w, lin2_w, vec1, vec2, out):
    f32, f32r = mybir.dt.float32, mybir.dt.float32r
    ACT, ALU, AX = mybir.ActivationFunctionType, mybir.AluOpType, mybir.AxisListType.X
    ds = bass.ds

    with ExitStack() as ctx:
        def sb(name, shape, dt=f32):
            return ctx.enter_context(nc.sbuf_tensor(name, shape, dt))

        def sem(name):
            return ctx.enter_context(nc.semaphore(name))

        HB = NB * P * 4
        base = (nc.sbuf_usable_end - 2 * HB) // 32 * 32
        h_hi = nc.alloc_sbuf_tensor_at("h_hi", [P, NB, P], f32r, offset=base)
        h_lo = nc.alloc_sbuf_tensor_at("h_lo", [P, NB, P], f32r, offset=base + HB)
        y = nc.alloc_sbuf_tensor_at("y", [P, H1, NT, TC], f32, offset=base)
        z = y[:, 0]
        X = sb("X", [P, NT, TC])
        rec_hi = sb("rec_hi", [P, NG, GB * 64], f32r)
        rec_lo = sb("rec_lo", [P, NG, GB * 64], f32r)
        c = sb("c", [P, NG, GB * 64])
        w_hi = sb("w_hi", [P, 7, 4 * P], f32r)
        w_lo = sb("w_lo", [P, 7, 4 * P], f32r)
        w_raw = c[:, :, :].rearrange("p g n -> p (g n)")[:, 0:7 * 4 * P].rearrange("p (m n) -> p m n", m=7)
        gates = sb("gates", [P, 2, 4, TC])
        f_in = sb("f_in", [P, TB, P])
        agg = sb("agg", [P, TC])
        pre1 = sb("pre1", [P, TB, P])
        h1 = sb("h1", [P, TB, P])
        u2 = sb("u2", [P, TB, P])
        h0_hi = rec_hi[:, NG - 1, :]
        h0_lo = rec_lo[:, NG - 1, :]
        hsum = pre1
        x_new = h1[:, :, :].rearrange("p b t -> p (b t)")
        zt = gates[:, 0, 0:2, :]
        adj_sb = sb("adj_sb", [P, 2, P])
        norm = sb("norm", [P, 2, P])
        ahatT = sb("ahatT", [P, P])
        ident = sb("ident", [P, P])
        gcn_w_sb = sb("gcn_w_sb", [P, 2, P])
        gcn_b_sb = sb("gcn_b_sb", [P, 2, P])
        row_bias = sb("row_bias", [P, P])
        lin1_sb = sb("lin1_sb", [P, H1 * P])
        lin2_sb = sb("lin2_sb", [P, H1, P])
        lstm_b_sb = sb("lstm_b_sb", [P, 2, SKIPS * 4])
        lstm_bias = sb("lstm_bias", [P, SKIPS * 4])
        vec1_sb = sb("vec1_sb", [P, 3, H1])
        vec2_sb = sb("vec2_sb", [P, 3, 1])
        mhalf = sb("mhalf", [P, TB])
        deg3 = sb("deg3", [P, 4])
        dinv = sb("dinv", [P, 1])
        st = sb("st", [P, TB, 6])
        half = sb("half", [P, 5, TB])
        var_eps = sb("var_eps", [P, TB])
        neg_mean = sb("neg_mean", [P, TB])
        rstd = sb("rstd", [P, TB])
        shift = sb("shift", [P, TB])
        st1 = sb("st1", [P, H1, NT, 6])
        mv1 = sb("mv1", [P, H1, 2])
        st2 = sb("st2", [P, NT, 6])
        mv2 = sb("mv2", [P, 1, 2])
        bn = sb("bn", [P, 2, 6, H1])
        assert nc.sbuf_base <= base, (nc.sbuf_base, base)
        ps = ctx.enter_context(nc.psum_tensor("ps", [P, 8, TC], f32))

        adj_loaded = sem("adj_loaded")
        gcn_loaded = sem("gcn_loaded")
        x_dma = [sem(f"x_dma{k}") for k in range(6)]
        x_ready = sem("x_ready")
        lstm_loaded = sem("lstm_loaded")
        lin_loaded = sem("lin_loaded")
        ident_ready = sem("ident_ready")
        mhalf_ready = sem("mhalf_ready")
        norm_steps = sem("norm_steps")
        deg_ready = sem("deg_ready")
        dinv_ready = sem("dinv_ready")
        scaled_ready = sem("scaled_ready")
        scaledT_done = sem("scaledT_done")
        ahatT_ready = sem("ahatT_ready")
        row_bias_done = sem("row_bias_done")
        row_bias_ready = sem("row_bias_ready")
        bias_ready = sem("bias_ready")
        w_hi_ready = sem("w_hi_ready")
        w_ready = sem("w_ready")
        ln_steps = sem("ln_steps")
        ln_stats = sem("ln_stats")
        rstd_done = sem("rstd_done")
        ln_ready = sem("ln_ready")
        f_ready = sem("f_ready")
        agg_done = sem("agg_done")
        agg_ready = sem("agg_ready")
        conv1_done = sem("conv1_done")
        pre1_ready = sem("pre1_ready")
        h1_ready = sem("h1_ready")
        u2_done = sem("u2_done")
        u2_ready = sem("u2_ready")
        conv2_done = sem("conv2_done")
        h0_hi_ready = sem("h0_hi_ready")
        h0_ready = sem("h0_ready")
        gate_done = sem("gate_done")
        ifg_ready = sem("ifg_ready")
        o_ready = sem("o_ready")
        ig_ready = sem("ig_ready")
        fc_ready = sem("fc_ready")
        c_ready = sem("c_ready")
        tanh_ready = sem("tanh_ready")
        hid_ready = sem("hid_ready")
        hid_hi_ready = sem("hid_hi_ready")
        hid_lo_ready = sem("hid_lo_ready")
        hsum_ready = sem("hsum_ready")
        back_done = sem("back_done")
        x_added = sem("x_added")
        x_kept = sem("x_kept")
        lin1_done = sem("lin1_done")
        y_ready = sem("y_ready")
        y_stats = sem("y_stats")
        bn_steps = sem("bn_steps")
        bn_var = sem("bn_var")
        bn_rstd = sem("bn_rstd")
        bn_ready = sem("bn_ready")
        yr_ready = sem("yr_ready")
        lin2_done = sem("lin2_done")
        z_ready = sem("z_ready")
        z_stats = sem("z_stats")
        zt_ready = sem("zt_ready")
        out_done = sem("out_done")
        out_ready = sem("out_ready")
        stored = sem("stored")

        X_CHUNKS = [1, 1, 2, 4, 4, 4]

        STEPS = [(p, s) for p in range(2, SKIPS + 1) for s in range(p)]

        def windows(p):
            return P // p

        def n_gates(s):
            return 3 if s == 0 else 4

        def gate_order(s):
            return [I_, G_, O_] if s == 0 else [I_, G_, F_, O_]

        GATES0, IFG0, FULL0, TANH0 = [3 * NT], [2 * NT], [0], [NT]
        for p_, s_ in STEPS:
            GATES0.append(GATES0[-1] + n_gates(s_) * NG)
            IFG0.append(IFG0[-1] + (n_gates(s_) - 1) * NG)
            FULL0.append(FULL0[-1] + (NG if s_ else 0))
        JOBS = NT + len(STEPS) * NG

        def positions(h, g, p, s, nb=GB):
            nw = windows(p)
            return h[:, ds(nb * g, nb), s:s + p * (nw - 1) + 1:p]

        def skewed_loop(engine, body, n_stages, lead=0):
            for i in range(n_stages):
                body(i, 0, i)
            with engine.Fori(n_stages, NT) as i:
                body(i, 0, n_stages - 1)
            for i in range(NT, NT + n_stages - 1):
                body(i, i - NT + 1, n_stages - 1)

        block = ctx.enter_context(nc.Block())

        @block.sync
        def _(sp):
            t = 0
            for k, n in enumerate(X_CHUNKS):
                sp.dma_start(X[:, t:t + n, :], x[:, t:t + n, :]).then_inc(x_dma[k], 16)
                t += n
            for k, n in enumerate(X_CHUNKS):
                sp.wait_ge(x_dma[k], 16)
                sp.sem_inc(x_ready, n)
            with sp.Fori(0, NT) as t:
                sp.wait_ge(out_ready, t + 1)
                sp.dma_start(out[:, ds(t, 1), :], X[:, ds(t, 1), :]).then_inc(stored, 16)
            sp.wait_ge(stored, 16 * NT)

        @block.gpsimd
        def _(pool):
            nc.gpsimd.memset(mhalf[:], -0.5).then_inc(mhalf_ready, 1)
            nc.gpsimd.memset(ident[:], 0.0).then_inc(ident_ready, 1)
            pool.wait_ge(ident_ready, 1)
            nc.gpsimd.affine_select(out=ident[:], in_=ident[:], compare_op=ALU.not_equal, fill=1.0, base=0,
                                    pattern=[[-1, P]], channel_multiplier=1).then_inc(ident_ready, 1)
            pool.wait_ge(mhalf_ready, 1)

            def layernorm_rstd(n):
                pool.wait_ge(ln_stats, n + 1)
                at_least(pool, f_ready, n)
                nc.gpsimd.tensor_tensor(rstd[:], var_eps[:], mhalf[:], ALU.pow).then_inc(rstd_done, 1)
                pool.wait_ge(rstd_done, n + 1)
                nc.gpsimd.tensor_tensor(shift[:], neg_mean[:], rstd[:], ALU.mult).then_inc(ln_ready, 1)

            def split_weights(m):
                if m == 0:
                    pool.wait_ge(lstm_loaded, 32)
                nc.gpsimd.tensor_copy(w_hi[:, m, :], w_raw[:, m, :]).then_inc(w_hi_ready, 1)
                pool.wait_ge(w_hi_ready, m + 1)
                nc.gpsimd.tensor_tensor(w_lo[:, m, :], w_raw[:, m, :], w_hi[:, m, :].bitcast(f32),
                                        ALU.subtract).then_inc(w_ready, 1)

            layernorm_rstd(0)
            pool.wait_ge(deg_ready, 1)
            nc.gpsimd.tensor_tensor(dinv[:], deg3[:, 3:4], mhalf[:, 0:1], ALU.pow).then_inc(dinv_ready, 1)

            def convolutions(i, first, last):
                if last >= 4:
                    t = i - 4
                    pool.wait_ge(hid_hi_ready, t + 1)
                    nc.gpsimd.tensor_tensor(h_lo[:, ds(TB * t, TB), :],
                                            gates[:, 1, O_, :].rearrange("p (b t) -> p b t", b=TB),
                                            h_hi[:, ds(TB * t, TB), :].bitcast(f32),
                                            ALU.subtract).then_inc(hid_lo_ready, 1)
                if first == 0 and not (isinstance(i, int) and i + 1 >= NT):
                    layernorm_rstd(i + 1)
                if isinstance(i, int) and i < 7:
                    split_weights(i)
            for i in range(7):
                convolutions(i, 0, min(i, 4))
            with pool.Fori(7, NT - 1) as i:
                convolutions(i, 0, 4)
            for i in range(NT - 1, NT + 4):
                convolutions(i, max(0, i - NT + 1), 4)

            for k, (p, s) in enumerate(STEPS):
                n = GB * windows(p)
                lo = rec_lo if s < p - 1 else h_lo
                hi = rec_hi if s < p - 1 else h_hi
                with pool.Fori(0, NG // 2) as i:
                    for q in range(2):
                        g = 2 * i + q
                        if s > 0:
                            pool.wait_ge(ifg_ready, IFG0[k] + 3 * g + 2)
                            nc.gpsimd.tensor_tensor(gates[:, q, I_, 0:n], gates[:, q, I_, 0:n],
                                                    gates[:, q, G_, 0:n], ALU.mult).then_inc(ig_ready, 1)
                        pool.wait_ge(hid_hi_ready, NT + NG * k + g + 1)
                        if s < p - 1:
                            lo_at, hi_at = lo[:, ds(g, 1), 0:n], hi[:, ds(g, 1), 0:n]
                            hid = gates[:, q, O_:O_ + 1, 0:n]
                        else:
                            lo_at, hi_at = positions(lo, g, p, s), positions(hi, g, p, s)
                            hid = gates[:, q, O_, 0:n].rearrange("p (b w) -> p b w", b=GB)
                        nc.gpsimd.tensor_tensor(lo_at, hid, hi_at.bitcast(f32),
                                                ALU.subtract).then_inc(hid_lo_ready, 1)

            pool.wait_ge(hid_lo_ready, JOBS)

            def gather(i, first, last):
                if first == 0:
                    if not (isinstance(i, int) and i == 0):
                        pool.wait_ge(back_done, i)
                    nc.gpsimd.tensor_tensor(hsum[:], h_hi[:, ds(TB * i, TB), :].bitcast(f32),
                                            h_lo[:, ds(TB * i, TB), :].bitcast(f32),
                                            ALU.add).then_inc(hsum_ready, 1)
                    pool.wait_ge(x_added, i + 1)
                    nc.gpsimd.tensor_copy(X[:, ds(i, 1), :], x_new[:, None, :]).then_inc(x_kept, 1)
                    layernorm_rstd(NT + i)
            skewed_loop(pool, gather, 1)

            for b in range(2):
                w = H1 if b == 0 else 1
                pool.wait_ge(bn_var, b + 1)
                nc.gpsimd.tensor_tensor(bn[:, b, 2, 0:w], bn[:, b, 0, 0:w], mhalf[:, 0:w],
                                        ALU.pow).then_inc(bn_rstd, 1)

        @block.scalar
        def _(act):
            act.dma_start(adj_sb[:, 0, :], adj).then_inc(adj_loaded, 16)
            act.dma_start(adj_sb[:, 1, :], adjT).then_inc(adj_loaded, 16)
            act.dma_start(gcn_w_sb[:], gcn_w).then_inc(gcn_loaded, 16)
            act.dma_start(gcn_b_sb[:], gcn_b.partition_broadcast(P)).then_inc(gcn_loaded, 16)
            act.dma_start(w_raw, lstm_w).then_inc(lstm_loaded, 16)
            act.dma_start(lstm_b_sb[:], lstm_b).then_inc(lstm_loaded, 16)
            act.dma_start(lin1_sb[:], lin1_w).then_inc(lin_loaded, 16)
            act.dma_start(lin2_sb[:], lin2_w).then_inc(lin_loaded, 16)
            act.dma_start(vec1_sb[:], vec1).then_inc(lin_loaded, 16)
            act.dma_start(vec2_sb[:], vec2).then_inc(lin_loaded, 16)

            def normalise(rows, n):
                act.wait_ge(ln_ready, n + 1)
                at_least(act, agg_done, n)
                for b in range(TB):
                    a = nc.scalar.activation(f_in[:, b:b + 1, :], rows[:, :, b * P:(b + 1) * P], ACT.Relu,
                                             bias=shift[:, b:b + 1], scale=rstd[:, b:b + 1])
                a.then_inc(f_ready, 1)

            def gate(k_bank, dst, func, bias, n, done):
                nc.scalar.activation(dst, ps[:, k_bank, 0:n], func, bias=bias).then_inc(done, 1)

            def func_of(g):
                return ACT.Tanh if g == G_ else ACT.Sigmoid

            normalise(X[:, 0:1, :], 0)

            def convolutions(i, first, last):
                if last >= 4:
                    t = i - 4
                    if isinstance(i, int) and i == 4:
                        act.wait_ge(bias_ready, 1)
                    at_least(act, hid_lo_ready, t)
                    for k, g in enumerate([I_, G_, O_]):
                        act.wait_ge(gate_done, 3 * t + k + 1)
                        gate(4 + k, gates[:, 1, g, :], func_of(g), lstm_bias[:, g:g + 1], TC,
                             o_ready if g == O_ else ifg_ready)
                    act.wait_ge(c_ready, t + 1)
                    nc.scalar.activation(gates[:, 1, G_, :], gates[:, 1, F_, :], ACT.Tanh).then_inc(tanh_ready, 1)
                if first <= 3 <= last:
                    t = i - 3
                    act.wait_ge(conv2_done, t + 1)
                    nc.scalar.activation(h0_hi, ps[:, 3, :], ACT.Relu).then_inc(h0_hi_ready, 1)
                if first <= 1 <= last:
                    t = i - 1
                    act.wait_ge(pre1_ready, t + 1)
                    nc.scalar.activation(h1[:], pre1[:], ACT.Relu).then_inc(h1_ready, 1)
                if first == 0:
                    act.wait_ge(agg_done, i + 1)
                    nc.scalar.activation(agg[:], ps[:, 0, :], ACT.Copy).then_inc(agg_ready, 1)
                    if not (isinstance(i, int) and i + 1 >= NT):
                        normalise(X[:, ds(i + 1, 1), :], i + 1)
            for i in range(5):
                convolutions(i, 0, i)
            with act.Fori(5, NT - 1) as i:
                convolutions(i, 0, 4)
            for i in range(NT - 1, NT + 4):
                convolutions(i, max(0, i - NT + 1), 4)

            for k, (p, s) in enumerate(STEPS):
                n = GB * windows(p)
                with act.Fori(0, NG // 2) as i:
                    for q in range(2):
                        g = 2 * i + q
                        job = NT + NG * k + g
                        act.wait_ge(hid_lo_ready, job - 1)
                        for m, gt in enumerate(gate_order(s)):
                            act.wait_ge(gate_done, GATES0[k] + n_gates(s) * g + m + 1)
                            gate(4 * q + gt, gates[:, q, gt, 0:n], func_of(gt),
                                 lstm_bias[:, 4 * (p - 1) + gt:4 * (p - 1) + gt + 1], n,
                                 o_ready if gt == O_ else ifg_ready)
                        act.wait_ge(c_ready, job + 1)
                        nc.scalar.activation(gates[:, q, G_:G_ + 1, 0:n], c[:, ds(g, 1), 0:n],
                                             ACT.Tanh).then_inc(tanh_ready, 1)

            def aggregate(i, first, last):
                if last >= 3:
                    t = i - 3
                    act.wait_ge(lin1_done, t + 1)
                    for k in range(H1):
                        nc.scalar.activation(y[:, k, ds(t, 1), :], ps[:, 2 + k:3 + k, :], ACT.Copy).then_inc(y_ready, 1)
                if first <= 2 <= last:
                    t = i - 2
                    act.wait_ge(agg_done, NT + t + 1)
                    nc.scalar.activation(agg[:], ps[:, 1, :], ACT.Copy).then_inc(agg_ready, 1)
                if first <= 1 <= last:
                    normalise(x_new[:, None, :], NT + i - 1)
            skewed_loop(act, aggregate, 4)

            act.wait_ge(bn_ready, 1)
            with act.Fori(0, NT) as t:
                for k in range(H1):
                    nc.scalar.activation(y[:, k, ds(t, 1), :], y[:, k, ds(t, 1), :], ACT.Relu,
                                         bias=bn[:, 0, 5, k:k + 1], scale=bn[:, 0, 3, k:k + 1]).then_inc(yr_ready, 1)

            act.wait_ge(bn_ready, 2)

            def scale_out(i, q):
                t = 2 * i + q
                at_least(act, out_done, t - 1)
                nc.scalar.activation(zt[:, q:q + 1, :], z[:, ds(t, 1), :], ACT.Identity,
                                     bias=bn[:, 1, 5, 0:1], scale=bn[:, 1, 3, 0:1]).then_inc(zt_ready, 1)
            scale_out(0, 0)
            scale_out(0, 1)
            with act.Fori(1, NT // 2) as i:
                scale_out(i, 0)
                scale_out(i, 1)

        @block.vector
        def _(dve):
            LN = 4

            def layernorm_stats(rows, n):
                for b in range(TB):
                    a = nc.vector.bn_stats(st[:, b, :], rows[..., b * P:(b + 1) * P])
                a.then_inc(ln_steps, 1)
                dve.wait_ge(ln_steps, LN * n + 1)
                nc.vector.tensor_tensor(half[:, 0, :], st[:, :, 1], st[:, :, 4], ALU.add)
                nc.vector.tensor_tensor(half[:, 1, :], st[:, :, 1], st[:, :, 4], ALU.subtract)
                nc.vector.tensor_tensor(half[:, 2, :], st[:, :, 2], st[:, :, 5], ALU.add).then_inc(ln_steps, 1)
                dve.wait_ge(ln_steps, LN * n + 2)
                nc.vector.scalar_tensor_tensor(half[:, 3, :], half[:, 1, :], 0.25, half[:, 1, :], ALU.mult, ALU.mult)
                nc.vector.tensor_scalar(half[:, 4, :], half[:, 2, :], 1.0 / P, EPS, ALU.mult, ALU.add
                                        ).then_inc(ln_steps, 1)
                dve.wait_ge(ln_steps, LN * n + 3)
                at_least(dve, ln_ready, n)
                nc.vector.tensor_scalar(neg_mean[:], half[:, 0, :], -0.5, None, ALU.mult).then_inc(ln_steps, 1)
                nc.vector.tensor_tensor(var_eps[:], half[:, 3, :], half[:, 4, :], ALU.add).then_inc(ln_stats, 1)

            dve.wait_ge(x_ready, 1)
            layernorm_stats(X[:, 0:1, :], 0)
            dve.wait_ge(adj_loaded, 32)
            dve.wait_ge(ident_ready, 2)
            for k in range(2):
                a = nc.vector.tensor_tensor(norm[:, k, :], adj_sb[:, k, :], ident[:], ALU.add)
            a.then_inc(norm_steps, 1)
            dve.wait_ge(norm_steps, 1)
            nc.vector.tensor_tensor(ahatT[:], norm[:, 0, :], ident[:], ALU.mult).then_inc(norm_steps, 1)
            nc.vector.reduce_sum(deg3[:, 0:2], norm[:], AX).then_inc(norm_steps, 1)
            dve.wait_ge(norm_steps, 3)
            nc.vector.reduce_sum(deg3[:, 2:3], ahatT[:], AX).then_inc(norm_steps, 1)
            dve.wait_ge(norm_steps, 4)
            nc.vector.tensor_tensor(deg3[:, 3:4], deg3[:, 0:1], deg3[:, 1:2], ALU.add).then_inc(norm_steps, 1)
            dve.wait_ge(norm_steps, 5)
            nc.vector.tensor_tensor(deg3[:, 3:4], deg3[:, 3:4], deg3[:, 2:3], ALU.subtract).then_inc(deg_ready, 1)
            dve.wait_ge(row_bias_done, 1)
            nc.vector.tensor_copy(row_bias[:], ps[:, 7, 0:P]).then_inc(row_bias_ready, 1)
            dve.wait_ge(dinv_ready, 1)
            nc.vector.tensor_scalar(norm[:, 0, :], norm[:, 0, :], dinv[:, 0:1], None, ALU.mult).then_inc(scaled_ready, 1)
            dve.wait_ge(lstm_loaded, 32)
            nc.vector.tensor_tensor(lstm_bias[:], lstm_b_sb[:, 0, :], lstm_b_sb[:, 1, :], ALU.add).then_inc(bias_ready, 1)
            dve.wait_ge(scaledT_done, 1)
            nc.vector.tensor_scalar(ahatT[:], ps[:, 6, 0:P], dinv[:, 0:1], None, ALU.mult).then_inc(ahatT_ready, 1)
            dve.wait_ge(row_bias_ready, 1)

            def convolutions(i, first, last):
                if first == 0 and not (isinstance(i, int) and i + 1 >= NT):
                    dve.wait_ge(x_ready, i + 2)
                if last >= 4:
                    t = i - 4
                    dve.wait_ge(ifg_ready, 2 * (t + 1))
                    nc.vector.tensor_tensor(gates[:, 1, F_, :], gates[:, 1, I_, :], gates[:, 1, G_, :],
                                            ALU.mult).then_inc(c_ready, 1)
                    dve.wait_ge(tanh_ready, t + 1)
                    dve.wait_ge(o_ready, t + 1)
                    nc.vector.tensor_tensor(gates[:, 1, O_, :], gates[:, 1, O_, :], gates[:, 1, G_, :],
                                            ALU.mult).then_inc(hid_ready, 1)
                    dve.wait_ge(hid_ready, t + 1)
                    nc.vector.tensor_copy(h_hi[:, ds(TB * t, TB), :],
                                          gates[:, 1, O_, :].rearrange("p (b t) -> p b t", b=TB)
                                          ).then_inc(hid_hi_ready, 1)
                if first <= 3 <= last:
                    t = i - 3
                    dve.wait_ge(h0_hi_ready, t + 1)
                    nc.vector.scalar_tensor_tensor(h0_lo, ps[:, 3, :], 0.0, h0_hi.bitcast(f32),
                                                   ALU.max, ALU.subtract).then_inc(h0_ready, 1)
                if first <= 2 <= last:
                    t = i - 2
                    dve.wait_ge(u2_done, t + 1)
                    nc.vector.tensor_tensor(u2[:], ps[:, 2, :].rearrange("p (b h) -> p b h", b=TB),
                                            gcn_b_sb[:, 1:2, :].to_broadcast([P, TB, P]),
                                            ALU.add).then_inc(u2_ready, 1)
                if first <= 1 <= last:
                    t = i - 1
                    dve.wait_ge(conv1_done, t + 1)
                    nc.vector.tensor_tensor(pre1[:], ps[:, 1, :].rearrange("p (b t) -> p b t", b=TB),
                                            row_bias[:, None, :].to_broadcast([P, TB, P]),
                                            ALU.add).then_inc(pre1_ready, 1)
                if first == 0 and not (isinstance(i, int) and i + 1 >= NT):
                    layernorm_stats(X[:, ds(i + 1, 1), :], i + 1)
            for i in range(5):
                convolutions(i, 0, i)
            with dve.Fori(5, NT - 1) as i:
                convolutions(i, 0, 4)
            for i in range(NT - 1, NT + 4):
                convolutions(i, max(0, i - NT + 1), 4)

            for k, (p, s) in enumerate(STEPS):
                n = GB * windows(p)
                hi = rec_hi if s < p - 1 else h_hi
                with dve.Fori(0, NG // 2) as i:
                    for q in range(2):
                        g = 2 * i + q
                        job = NT + NG * k + g
                        c_at = c[:, ds(g, 1), 0:n]
                        if s == 0:
                            dve.wait_ge(ifg_ready, IFG0[k] + 2 * g + 2)
                            nc.vector.tensor_tensor(c_at, gates[:, q, I_:I_ + 1, 0:n], gates[:, q, G_:G_ + 1, 0:n],
                                                    ALU.mult).then_inc(c_ready, 1)
                        else:
                            dve.wait_ge(ifg_ready, IFG0[k] + 3 * g + 3)
                            nc.vector.tensor_tensor(gates[:, q, F_:F_ + 1, 0:n], gates[:, q, F_:F_ + 1, 0:n], c_at,
                                                    ALU.mult).then_inc(fc_ready, 1)
                            dve.wait_ge(fc_ready, FULL0[k] + g + 1)
                            dve.wait_ge(ig_ready, FULL0[k] + g + 1)
                            nc.vector.tensor_tensor(c_at, gates[:, q, F_:F_ + 1, 0:n], gates[:, q, I_:I_ + 1, 0:n],
                                                    ALU.add).then_inc(c_ready, 1)
                        dve.wait_ge(o_ready, job + 1)
                        dve.wait_ge(tanh_ready, job + 1)
                        nc.vector.tensor_tensor(gates[:, q, O_, 0:n], gates[:, q, O_, 0:n], gates[:, q, G_, 0:n],
                                                ALU.mult).then_inc(hid_ready, 1)
                        dve.wait_ge(hid_ready, job + 1)
                        if s < p - 1:
                            nc.vector.tensor_copy(hi[:, ds(g, 1), 0:n], gates[:, q, O_:O_ + 1, 0:n]
                                                  ).then_inc(hid_hi_ready, 1)
                        else:
                            nc.vector.tensor_copy(positions(hi, g, p, s),
                                                  gates[:, q, O_, 0:n].rearrange("p (b w) -> p b w", b=GB)
                                                  ).then_inc(hid_hi_ready, 1)

            def aggregate(i, first, last):
                if last >= 3:
                    dve.wait_ge(y_ready, H1 * (i - 3) + H1)
                if first == 0:
                    dve.wait_ge(back_done, i + 1)
                    if not (isinstance(i, int) and i == 0):
                        dve.wait_ge(f_ready, NT + i)
                        dve.wait_ge(x_kept, i)
                    nc.vector.tensor_tensor(x_new[:, None, :], ps[:, 0:1, :], X[:, ds(i, 1), :],
                                            ALU.add).then_inc(x_added, 1)
                if last >= 3:
                    t = i - 3
                    for k in range(H1):
                        nc.vector.bn_stats(st1[:, k, ds(t, 1), :], y[:, k, ds(t, 1), :]).then_inc(y_stats, 1)
                if first == 0:
                    dve.wait_ge(x_added, i + 1)
                    layernorm_stats(x_new, NT + i)
            skewed_loop(dve, aggregate, 4)

            def batchnorm(b, width, vec, mean_var, steps):
                w = slice(0, width)
                nc.vector.tensor_tensor(bn[:, b, 1, w], mean_var[:, :, 0], vec[:, 0, :], ALU.add).then_inc(bn_steps, 1)
                nc.vector.tensor_scalar(bn[:, b, 0, w], mean_var[:, :, 1], EPS, None, ALU.add).then_inc(bn_var, 1)
                dve.wait_ge(bn_steps, steps + 1)
                nc.vector.tensor_tensor(bn[:, b, 4, w], vec[:, 0, :], bn[:, b, 1, w], ALU.subtract
                                        ).then_inc(bn_steps, 1)
                dve.wait_ge(bn_rstd, b + 1)
                nc.vector.tensor_tensor(bn[:, b, 3, w], bn[:, b, 2, w], vec[:, 1, :], ALU.mult).then_inc(bn_steps, 1)
                dve.wait_ge(bn_steps, steps + 3)
                nc.vector.tensor_tensor(bn[:, b, 1, w], bn[:, b, 4, w], bn[:, b, 3, w], ALU.mult).then_inc(bn_steps, 1)
                dve.wait_ge(bn_steps, steps + 4)
                nc.vector.tensor_tensor(bn[:, b, 5, w], bn[:, b, 1, w], vec[:, 2, :], ALU.add).then_inc(bn_ready, 1)

            dve.wait_ge(lin_loaded, 64)
            dve.wait_ge(y_stats, H1 * NT)
            for k in range(H1):
                a = nc.vector.bn_aggr(mv1[:, k, :], st1[:, k, :, :].rearrange("p t s -> p (t s)"))
            a.then_inc(bn_steps, 1)
            dve.wait_ge(bn_steps, 1)
            batchnorm(0, H1, vec1_sb, mv1, 1)

            with dve.Fori(0, NT // 2) as i:
                for q in range(2):
                    t = 2 * i + q
                    dve.wait_ge(lin2_done, t + 1)
                    nc.vector.tensor_copy(z[:, ds(t, 1), :], ps[:, 4 + q:5 + q, :]).then_inc(z_ready, 1)
                    nc.vector.bn_stats(st2[:, ds(t, 1), :], ps[:, 4 + q:5 + q, :]).then_inc(z_stats, 1)
            dve.wait_ge(z_stats, NT)
            nc.vector.bn_aggr(mv2[:, 0, :], st2[:, :, :].rearrange("p t s -> p (t s)")).then_inc(bn_steps, 1)
            dve.wait_ge(bn_steps, 6)
            batchnorm(1, 1, vec2_sb, mv2, 6)

            with dve.Fori(0, NT // 2) as i:
                for q in range(2):
                    t = 2 * i + q
                    dve.wait_ge(out_done, t + 1)
                    nc.vector.tensor_tensor(X[:, ds(t, 1), :], ps[:, 6 + q:7 + q, :], X[:, ds(t, 1), :],
                                            ALU.add).then_inc(out_ready, 1)

        @block.tensor
        def _(pe):
            adjT_mov = adj_sb[:, 1, :]

            pe.wait_ge(adj_loaded, 32)
            pe.wait_ge(gcn_loaded, 32)
            nc.tensor.matmul(ps[:, 7, 0:P], gcn_b_sb[:, 0, :], adjT_mov, start=True, stop=True).then_inc(row_bias_done, 1)
            pe.wait_ge(ident_ready, 2)
            pe.wait_ge(scaled_ready, 1)
            nc.tensor.transpose(ps[:, 6, 0:P], norm[:, 0, :], ident[:]).then_inc(scaledT_done, 1)
            pe.wait_ge(ahatT_ready, 1)
            pe.wait_ge(row_bias_ready, 1)

            def data_times(bank, data, moving, done):
                for b in range(TB):
                    m = nc.tensor.matmul(ps[:, bank, b * P:(b + 1) * P], data[:, b, :], moving, start=True, stop=True)
                m.then_inc(done, 1)

            def split_product(out_at, m, gt, hi, lo, start, stop):
                w = slice(gt * P, (gt + 1) * P)
                nc.tensor.matmul(out_at, w_hi[:, m, w], hi, start=start, stop=False)
                nc.tensor.matmul(out_at, w_hi[:, m, w], lo, start=False, stop=False)
                return nc.tensor.matmul(out_at, w_lo[:, m, w], hi, start=False, stop=stop)

            def convolutions(i, first, last):
                if last >= 4:
                    t = i - 4
                    if isinstance(i, int) and i == 4:
                        pe.wait_ge(w_ready, 1)
                    pe.wait_ge(h0_ready, t + 1)
                    at_least(pe, o_ready, t)
                    for k, gt in enumerate([I_, G_, O_]):
                        split_product(ps[:, 4 + k, :], 0, gt, h0_hi, h0_lo, True, True).then_inc(gate_done, 1)
                if first <= 3 <= last:
                    pe.wait_ge(u2_ready, i - 3 + 1)
                    data_times(3, u2, adjT_mov, conv2_done)
                if first <= 2 <= last:
                    pe.wait_ge(h1_ready, i - 2 + 1)
                    data_times(2, h1, gcn_w_sb[:, 1, :], u2_done)
                if first <= 1 <= last:
                    pe.wait_ge(agg_ready, i - 1 + 1)
                    nc.tensor.matmul(ps[:, 1, :], gcn_w_sb[:, 0, :], agg[:], start=True, stop=True
                                     ).then_inc(conv1_done, 1)
                if first == 0:
                    pe.wait_ge(f_ready, i + 1)
                    data_times(0, f_in, adjT_mov, agg_done)
            skewed_loop(pe, convolutions, 5)

            pe.wait_ge(w_ready, 7)
            for k, (p, s) in enumerate(STEPS):
                n = GB * windows(p)
                m_ih = 2 * p - 3
                with pe.Fori(0, NG // 2) as i:
                    for q in range(2):
                        g = 2 * i + q
                        if k == 0:
                            pe.wait_ge(hid_lo_ready, 2 * g + 2)
                        else:
                            pe.wait_ge(hid_lo_ready, NT + NG * (k - 1) + g + 1)
                        pe.wait_ge(o_ready, NT + NG * k + g - 1)
                        for gt in gate_order(s):
                            bank = ps[:, 4 * q + gt, 0:n]
                            a = split_product(bank, m_ih, gt, positions(h_hi, g, p, s), positions(h_lo, g, p, s),
                                              True, s == 0)
                            if s > 0:
                                a = split_product(bank, m_ih + 1, gt, rec_hi[:, ds(g, 1), 0:n],
                                                  rec_lo[:, ds(g, 1), 0:n], False, True)
                            a.then_inc(gate_done, 1)

            pe.wait_ge(lin_loaded, 64)
            pe.wait_ge(o_ready, JOBS)

            def aggregate(i, first, last):
                if last >= 3:
                    t = i - 3
                    pe.wait_ge(agg_ready, NT + t + 1)
                    at_least(pe, y_ready, H1 * t)
                    for k in range(H1):
                        m = nc.tensor.matmul(ps[:, 2 + k, :], lin1_sb[:, k * P:(k + 1) * P], agg[:],
                                             start=True, stop=True)
                    m.then_inc(lin1_done, 1)
                if first <= 2 <= last:
                    pe.wait_ge(f_ready, NT + i - 2 + 1)
                    data_times(1, f_in, ahatT[:], agg_done)
                if first == 0:
                    pe.wait_ge(hsum_ready, i + 1)
                    at_least(pe, x_added, i)
                    for b in range(TB):
                        m = nc.tensor.transpose(ps[:, 0, b * P:(b + 1) * P], hsum[:, b, :], ident[:])
                    m.then_inc(back_done, 1)
            skewed_loop(pe, aggregate, 4)

            def second_linear(i, q):
                t = 2 * i + q
                pe.wait_ge(yr_ready, H1 * t + H1)
                at_least(pe, z_stats, t - 1)
                for k in range(H1):
                    m = nc.tensor.matmul(ps[:, 4 + q:5 + q, :], lin2_sb[:, k, :], y[:, k, ds(t, 1), :],
                                         start=(k == 0), stop=(k == H1 - 1))
                m.then_inc(lin2_done, 1)
            second_linear(0, 0)
            second_linear(0, 1)
            with pe.Fori(1, NT // 2) as i:
                second_linear(i, 0)
                second_linear(i, 1)

            def turn_out(i, q):
                t = 2 * i + q
                pe.wait_ge(zt_ready, t + 1)
                at_least(pe, out_ready, t - 1)
                for b in range(TB):
                    m = nc.tensor.transpose(ps[:, 6 + q, b * P:(b + 1) * P], zt[:, q, b * P:(b + 1) * P], ident[:])
                m.then_inc(out_done, 1)
            turn_out(0, 0)
            turn_out(0, 1)
            with pe.Fori(1, NT // 2) as i:
                turn_out(i, 0)
                turn_out(i, 1)


def kernel(**inputs):
    import numpy as np
    import concourse.bacc as bacc
    from concourse.bass_utils import run_bass_kernel_spmd

    def a(name):
        return np.asarray(inputs[name])

    wih, whh = a("L0_gnn_Wih"), a("L0_gnn_Whh")
    order = [(wih, 0)] + [(w, p) for p in range(1, SKIPS) for w in (wih, whh)]
    arrays = {
        "x": a("x").transpose(1, 0, 2).reshape(P, NT, TC),
        "adj": a("adj"),
        "adjT": a("adj").T,
        "gcn_w": np.stack([a("L0_gnn_Wg0"), a("L0_gnn_Wg1")], 1),
        "gcn_b": np.stack([a("L0_gnn_bg0"), a("L0_gnn_bg1")], 0),
        "lstm_w": np.stack([w[p].T for w, p in order], 1),
        "lstm_b": np.stack([a(n).reshape(SKIPS * 4, P).T for n in ("L0_gnn_bih", "L0_gnn_bhh")], 1),
        "lin1_w": a("L1_gnn_W1").T,
        "lin2_w": a("L1_gnn_W2").T.reshape(H1, P, P).transpose(1, 0, 2),
        "vec1": np.stack([a(n).reshape(H1, P).T for n in ("L1_gnn_b1", "L1_gnn_g1", "L1_gnn_be1")], 1),
        "vec2": np.stack([a(n).reshape(1, P).T for n in ("L1_gnn_b2", "L1_gnn_g2", "L1_gnn_be2")], 1),
    }
    arrays = {k: np.ascontiguousarray(v) for k, v in arrays.items()}
    nc = bacc.Bacc("TRN2", target_bir_lowering=False, num_devices=1)
    args = [nc.dram_tensor(k, v.shape, mybir.dt.float32, kind="ExternalInput").ap() for k, v in arrays.items()]
    out = nc.dram_tensor("out", (P, NT, TC), mybir.dt.float32, kind="ExternalOutput").ap()
    gnn_kernel(nc, *args, out)
    r = run_bass_kernel_spmd(nc, [arrays], core_ids=[0]).results[0]["out"]
    return np.ascontiguousarray(r.reshape(P, NB, P).transpose(1, 0, 2))
```

```python
import concourse.bass as bass
from concourse import mybir
from contextlib import ExitStack

P = 128
NB = 64
TB = 4
NT = NB // TB
TC = TB * P
GB = 8
NG = NB // GB
SKIPS = 4
EPS = 1e-5
I_, F_, G_, O_ = range(4)
H1 = 2


def at_least(engine, sem, value):
    if isinstance(value, int) and value < 1:
        return
    engine.wait_ge(sem, value)


def gnn_kernel(nc, x, graph, gcn_b, lstm_w, lstm_b, lin1_w, lin2_w, vec1, vec2, out):
    f32, f32r = mybir.dt.float32, mybir.dt.float32r
    ACT, ALU, AX = mybir.ActivationFunctionType, mybir.AluOpType, mybir.AxisListType.X
    ds = bass.ds

    with ExitStack() as ctx:
        def sb(name, shape, dt=f32):
            return ctx.enter_context(nc.sbuf_tensor(name, shape, dt))

        def sem(name):
            return ctx.enter_context(nc.semaphore(name))

        HB = NB * P * 4
        base = (nc.sbuf_usable_end - 2 * HB) // 32 * 32
        h_hi = nc.alloc_sbuf_tensor_at("h_hi", [P, NB, P], f32r, offset=base)
        h_lo = nc.alloc_sbuf_tensor_at("h_lo", [P, NB, P], f32r, offset=base + HB)
        y = nc.alloc_sbuf_tensor_at("y", [P, H1, NT, TC], f32, offset=base)
        z = y[:, 0]
        X = sb("X", [P, NT, TC])
        rec_hi = sb("rec_hi", [P, NG, GB * 64], f32r)
        rec_lo = sb("rec_lo", [P, NG, GB * 64], f32r)
        c = sb("c", [P, NG, GB * 64])
        w_hi = sb("w_hi", [P, 7, 4 * P], f32r)
        w_lo = sb("w_lo", [P, 7, 4 * P], f32r)
        w_raw = c[:, :, :].rearrange("p g n -> p (g n)")[:, 0:7 * 4 * P].rearrange("p (m n) -> p m n", m=7)
        gates = sb("gates", [P, 2, 4, TC])
        cell1, tanh1, hid1 = (gates[:, 0, k, :] for k in (F_, G_, O_))
        f_in = sb("f_in", [P, TB, P])
        agg = sb("agg", [P, TC])
        pre1 = sb("pre1", [P, TB, P])
        h1 = sb("h1", [P, TB, P])
        u2 = sb("u2", [P, TB, P])
        h0_hi = rec_hi[:, NG - 1, :]
        h0_lo = rec_lo[:, NG - 1, :]
        hsum = pre1
        xn = c[:, NG - 1:NG, :]
        zt = gates[:, 0, 0:2, :]
        graph_sb = sb("graph_sb", [P, 4, P])
        adj_sb, gcn_w_sb = graph_sb[:, 0:2, :], graph_sb[:, 2:4, :]
        norm = sb("norm", [P, 2, P])
        ahatT = sb("ahatT", [P, P])
        ident = sb("ident", [P, P])
        gcn_b_sb = sb("gcn_b_sb", [P, 2, P])
        row_bias = sb("row_bias", [P, P])
        lin1_sb = sb("lin1_sb", [P, H1 * P])
        lin2_sb = sb("lin2_sb", [P, H1, P])
        lstm_b_sb = sb("lstm_b_sb", [P, 2, SKIPS * 4])
        lstm_bias = sb("lstm_bias", [P, SKIPS * 4])
        vec1_sb = sb("vec1_sb", [P, 3, H1])
        vec2_sb = sb("vec2_sb", [P, 3, 1])
        mhalf = sb("mhalf", [P, TB])
        deg3 = sb("deg3", [P, 4])
        dinv = sb("dinv", [P, 1])
        st = sb("st", [P, TB, 6])
        half = sb("half", [P, 5, TB])
        var_eps = sb("var_eps", [P, TB])
        neg_mean = sb("neg_mean", [P, TB])
        rstd = sb("rstd", [P, TB])
        shift = sb("shift", [P, TB])
        st1 = sb("st1", [P, H1, NT, 6])
        mv1 = sb("mv1", [P, H1, 2])
        st2 = sb("st2", [P, NT, 6])
        mv2 = sb("mv2", [P, 1, 2])
        bn = sb("bn", [P, 2, 6, H1])
        assert nc.sbuf_base <= base, (nc.sbuf_base, base)
        ps = ctx.enter_context(nc.psum_tensor("ps", [P, 8, TC], f32))

        graph_loaded = sem("graph_loaded")
        x_dma = [sem(f"x_dma{k}") for k in range(6)]
        x_ready = sem("x_ready")
        lstm_loaded = sem("lstm_loaded")
        lin_loaded = sem("lin_loaded")
        ident_ready = sem("ident_ready")
        mhalf_ready = sem("mhalf_ready")
        norm_steps = sem("norm_steps")
        deg_ready = sem("deg_ready")
        dinv_ready = sem("dinv_ready")
        scaled_ready = sem("scaled_ready")
        scaledT_done = sem("scaledT_done")
        ahatT_ready = sem("ahatT_ready")
        row_bias_done = sem("row_bias_done")
        row_bias_ready = sem("row_bias_ready")
        bias_ready = sem("bias_ready")
        w_hi_ready = sem("w_hi_ready")
        w_ready = sem("w_ready")
        ln_steps = sem("ln_steps")
        ln_stats = sem("ln_stats")
        rstd_done = sem("rstd_done")
        ln_ready = sem("ln_ready")
        xn_ready = sem("xn_ready")
        f_ready = sem("f_ready")
        agg_done = sem("agg_done")
        agg_ready = sem("agg_ready")
        conv1_done = sem("conv1_done")
        pre1_ready = sem("pre1_ready")
        h1_ready = sem("h1_ready")
        u2_done = sem("u2_done")
        u2_ready = sem("u2_ready")
        conv2_done = sem("conv2_done")
        h0_hi_ready = sem("h0_hi_ready")
        h0_ready = sem("h0_ready")
        gate_done = sem("gate_done")
        ifg_ready = sem("ifg_ready")
        o_ready = sem("o_ready")
        ig_ready = sem("ig_ready")
        fc_ready = sem("fc_ready")
        c_ready = sem("c_ready")
        tanh_ready = sem("tanh_ready")
        hid_ready = sem("hid_ready")
        hid_hi_ready = sem("hid_hi_ready")
        hid_lo_ready = sem("hid_lo_ready")
        hsum_ready = sem("hsum_ready")
        back_done = sem("back_done")
        x_added = sem("x_added")
        lin1_done = sem("lin1_done")
        y_ready = sem("y_ready")
        y_stats = sem("y_stats")
        bn_steps = sem("bn_steps")
        bn_var = sem("bn_var")
        bn_rstd = sem("bn_rstd")
        bn_ready = sem("bn_ready")
        yr_ready = sem("yr_ready")
        lin2_done = sem("lin2_done")
        z_ready = sem("z_ready")
        z_stats = sem("z_stats")
        zt_ready = sem("zt_ready")
        out_done = sem("out_done")
        out_ready = sem("out_ready")
        stored = sem("stored")

        X_CHUNKS = [1, 1, 2, 4, 4, 4]

        STEPS = [(p, s) for p in range(2, SKIPS + 1) for s in range(p)]

        def windows(p):
            return P // p

        def n_gates(s):
            return 3 if s == 0 else 4

        def gate_order(s):
            return [I_, G_, O_] if s == 0 else [I_, G_, F_, O_]

        GATES0, IFG0, FULL0, TANH0 = [3 * NT], [2 * NT], [0], [NT]
        for p_, s_ in STEPS:
            GATES0.append(GATES0[-1] + n_gates(s_) * NG)
            IFG0.append(IFG0[-1] + (n_gates(s_) - 1) * NG)
            FULL0.append(FULL0[-1] + (NG if s_ else 0))
        JOBS = NT + len(STEPS) * NG

        def positions(h, g, p, s, nb=GB):
            nw = windows(p)
            return h[:, ds(nb * g, nb), s:s + p * (nw - 1) + 1:p]

        def skewed_loop(engine, body, n_stages, lead=0):
            for i in range(n_stages):
                body(i, 0, i)
            with engine.Fori(n_stages, NT) as i:
                body(i, 0, n_stages - 1)
            for i in range(NT, NT + n_stages - 1):
                body(i, i - NT + 1, n_stages - 1)

        def lstm_slots(engine, slot):
            prev = None
            for k in range(len(STEPS)):
                slot(k, 0, 0, prev)
                slot(k, 0, 1, (k, 0, 0))
                with engine.Fori(1, NG // 2) as i:
                    slot(k, i, 0, (k, i - 1, 1))
                    slot(k, i, 1, (k, i, 0))
                prev = (k, NG // 2 - 1, 1)
            return prev

        block = ctx.enter_context(nc.Block())

        @block.sync
        def _(sp):
            t = 0
            for k, n in enumerate(X_CHUNKS):
                sp.dma_start(X[:, t:t + n, :], x[:, t:t + n, :]).then_inc(x_dma[k], 16)
                t += n
                if k == 0:
                    sp.dma_start(graph_sb[:], graph).then_inc(graph_loaded, 16)
                    sp.dma_start(gcn_b_sb[:], gcn_b.partition_broadcast(P)).then_inc(graph_loaded, 16)
                if k == 2:
                    sp.dma_start(w_raw, lstm_w).then_inc(lstm_loaded, 16)
                    sp.dma_start(lstm_b_sb[:], lstm_b).then_inc(lstm_loaded, 16)
            sp.dma_start(lin1_sb[:], lin1_w).then_inc(lin_loaded, 16)
            sp.dma_start(lin2_sb[:], lin2_w).then_inc(lin_loaded, 16)
            sp.dma_start(vec1_sb[:], vec1).then_inc(lin_loaded, 16)
            sp.dma_start(vec2_sb[:], vec2).then_inc(lin_loaded, 16)
            for k, n in enumerate(X_CHUNKS):
                sp.wait_ge(x_dma[k], 16)
                sp.sem_inc(x_ready, n)
            with sp.Fori(0, NT) as t:
                sp.wait_ge(out_ready, t + 1)
                sp.dma_start(out[:, ds(t, 1), :], X[:, ds(t, 1), :]).then_inc(stored, 16)
            sp.wait_ge(stored, 16 * NT)

        @block.gpsimd
        def _(pool):
            nc.gpsimd.memset(mhalf[:], -0.5).then_inc(mhalf_ready, 1)
            nc.gpsimd.memset(ident[:], 0.0).then_inc(ident_ready, 1)
            pool.wait_ge(ident_ready, 1)
            nc.gpsimd.affine_select(out=ident[:], in_=ident[:], compare_op=ALU.not_equal, fill=1.0, base=0,
                                    pattern=[[-1, P]], channel_multiplier=1).then_inc(ident_ready, 1)
            pool.wait_ge(mhalf_ready, 1)

            def layernorm_rstd(n, used):
                pool.wait_ge(ln_stats, n + 1)
                at_least(pool, used, n)
                nc.gpsimd.tensor_tensor(rstd[:], var_eps[:], mhalf[:], ALU.pow).then_inc(rstd_done, 1)
                pool.wait_ge(rstd_done, n + 1)
                nc.gpsimd.tensor_tensor(shift[:], neg_mean[:], rstd[:], ALU.mult).then_inc(ln_ready, 1)

            def weights_lo(m):
                pool.wait_ge(w_hi_ready, m + 1)
                nc.gpsimd.tensor_tensor(w_lo[:, m, :], w_raw[:, m, :], w_hi[:, m, :].bitcast(f32),
                                        ALU.subtract).then_inc(w_ready, 1)

            layernorm_rstd(0, xn_ready)
            pool.wait_ge(deg_ready, 1)
            nc.gpsimd.tensor_tensor(dinv[:], deg3[:, 3:4], mhalf[:, 0:1], ALU.pow).then_inc(dinv_ready, 1)

            def convolutions(i, first, last):
                if first == 0 and not (isinstance(i, int) and i + 1 >= NT):
                    layernorm_rstd(i + 1, xn_ready)
                if first <= 4 <= last:
                    t = i - 4
                    pool.wait_ge(ifg_ready, 2 * (t + 1))
                    at_least(pool, tanh_ready, t)
                    nc.gpsimd.tensor_tensor(cell1, gates[:, 1, I_, :], gates[:, 1, G_, :],
                                            ALU.mult).then_inc(c_ready, 1)
                if last >= 5:
                    t = i - 5
                    pool.wait_ge(hid_hi_ready, t + 1)
                    nc.gpsimd.tensor_tensor(h_lo[:, ds(TB * t, TB), :],
                                            hid1.rearrange("p (b t) -> p b t", b=TB),
                                            h_hi[:, ds(TB * t, TB), :].bitcast(f32),
                                            ALU.subtract).then_inc(hid_lo_ready, 1)
                if isinstance(i, int) and i < 4:
                    for m in range(2 * i, min(2 * i + 2, 7)):
                        weights_lo(m)
            for i in range(6):
                convolutions(i, 0, i)
            with pool.Fori(6, NT - 1) as i:
                convolutions(i, 0, 5)
            for i in range(NT - 1, NT + 5):
                convolutions(i, max(0, i - NT + 1), 5)

            def low_part(k, i, q):
                p, s = STEPS[k]
                n, g = GB * windows(p), 2 * i + q
                pool.wait_ge(hid_hi_ready, NT + NG * k + g + 1)
                if s < p - 1:
                    lo_at, hi_at = rec_lo[:, ds(g, 1), 0:n], rec_hi[:, ds(g, 1), 0:n]
                    hid = gates[:, q, O_:O_ + 1, 0:n]
                else:
                    lo_at, hi_at = positions(h_lo, g, p, s), positions(h_hi, g, p, s)
                    hid = gates[:, q, O_, 0:n].rearrange("p (b w) -> p b w", b=GB)
                nc.gpsimd.tensor_tensor(lo_at, hid, hi_at.bitcast(f32), ALU.subtract).then_inc(hid_lo_ready, 1)

            def slot(k, i, q, prev):
                p, s = STEPS[k]
                n, g = GB * windows(p), 2 * i + q
                if s > 0:
                    pool.wait_ge(ifg_ready, IFG0[k] + 3 * g + 2)
                    nc.gpsimd.tensor_tensor(gates[:, q, I_, 0:n], gates[:, q, I_, 0:n],
                                            gates[:, q, G_, 0:n], ALU.mult).then_inc(ig_ready, 1)
                if prev:
                    low_part(*prev)
            low_part(*lstm_slots(pool, slot))

            pool.wait_ge(hid_lo_ready, JOBS)

            def gather(t):
                nc.gpsimd.tensor_tensor(hsum[:], h_hi[:, ds(TB * t, TB), :].bitcast(f32),
                                        h_lo[:, ds(TB * t, TB), :].bitcast(f32), ALU.add).then_inc(hsum_ready, 1)

            gather(0)
            pool.wait_ge(back_done, 1)
            gather(1)
            with pool.Fori(1, NT - 1) as i:
                pool.wait_ge(back_done, i + 1)
                gather(i + 1)
                layernorm_rstd(NT + i - 1, f_ready)
            layernorm_rstd(2 * NT - 2, f_ready)
            layernorm_rstd(2 * NT - 1, f_ready)

            for b in range(2):
                w = H1 if b == 0 else 1
                pool.wait_ge(bn_var, b + 1)
                nc.gpsimd.tensor_tensor(bn[:, b, 2, 0:w], bn[:, b, 0, 0:w], mhalf[:, 0:w],
                                        ALU.pow).then_inc(bn_rstd, 1)

        @block.scalar
        def _(act):
            def weights_hi(m):
                if m == 0:
                    act.wait_ge(lstm_loaded, 32)
                nc.scalar.activation(w_hi[:, m, :], w_raw[:, m, :], ACT.Copy).then_inc(w_hi_ready, 1)

            def normalise(rows, n):
                act.wait_ge(ln_ready, n + 1)
                act.wait_ge(agg_done, n)
                for b in range(TB):
                    a = nc.scalar.activation(f_in[:, b:b + 1, :], rows[:, :, b * P:(b + 1) * P], ACT.Relu,
                                             bias=shift[:, b:b + 1], scale=rstd[:, b:b + 1])
                a.then_inc(f_ready, 1)

            def gate(k_bank, dst, func, bias, n, done):
                nc.scalar.activation(dst, ps[:, k_bank, 0:n], func, bias=bias).then_inc(done, 1)

            def func_of(g):
                return ACT.Tanh if g == G_ else ACT.Sigmoid

            def relu_in(t):
                act.wait_ge(xn_ready, t + 1)
                at_least(act, agg_done, t)
                nc.scalar.activation(f_in[:], xn.rearrange("p a (b d) -> p (a b) d", b=TB), ACT.Relu
                                     ).then_inc(f_ready, 1)

            def convolutions(i, first, last):
                if first <= 2 <= last:
                    act.wait_ge(pre1_ready, i - 2 + 1)
                    nc.scalar.activation(h1[:], pre1[:], ACT.Relu).then_inc(h1_ready, 1)
                if first <= 1 <= last:
                    act.wait_ge(agg_done, i - 1 + 1)
                    nc.scalar.activation(agg[:], ps[:, 0, :], ACT.Copy).then_inc(agg_ready, 1)
                if last >= 5:
                    t = i - 5
                    act.wait_ge(c_ready, t + 1)
                    at_least(act, hid_ready, t)
                    nc.scalar.activation(tanh1, cell1, ACT.Tanh).then_inc(tanh_ready, 1)
                if first == 0:
                    relu_in(i)
                if first <= 4 <= last:
                    t = i - 4
                    if isinstance(i, int) and i == 4:
                        act.wait_ge(bias_ready, 1)
                    for k, g in enumerate([I_, G_, O_]):
                        at_least(act, hid_ready if g == O_ else c_ready, t)
                        act.wait_ge(gate_done, 3 * t + k + 1)
                        gate(4 + k, gates[:, 1, g, :], func_of(g), lstm_bias[:, g:g + 1], TC,
                             o_ready if g == O_ else ifg_ready)
                if first <= 3 <= last:
                    act.wait_ge(conv2_done, i - 3 + 1)
                    nc.scalar.activation(h0_hi, ps[:, 3, :], ACT.Relu).then_inc(h0_hi_ready, 1)
                if last >= 5:
                    t = i - 5
                    act.wait_ge(hid_ready, t + 1)
                    nc.scalar.activation(h_hi[:, ds(TB * t, TB), :], hid1.rearrange("p (b t) -> p b t", b=TB),
                                         ACT.Copy).then_inc(hid_hi_ready, 1)
                if isinstance(i, int) and i < 4:
                    for m in range(2 * i, min(2 * i + 2, 7)):
                        weights_hi(m)
            skewed_loop(act, convolutions, 6)

            def tanh_cell(k, i, q):
                n, g = GB * windows(STEPS[k][0]), 2 * i + q
                act.wait_ge(c_ready, NT + NG * k + g + 1)
                nc.scalar.activation(gates[:, q, G_:G_ + 1, 0:n], c[:, ds(g, 1), 0:n], ACT.Tanh).then_inc(tanh_ready, 1)

            def slot(k, i, q, prev):
                p, s = STEPS[k]
                n, g = GB * windows(p), 2 * i + q
                job = NT + NG * k + g
                for m, gt in enumerate(gate_order(s)):
                    act.wait_ge({I_: c_ready, G_: hid_ready, F_: c_ready, O_: hid_lo_ready}[gt],
                                job if prev is None else job - 1)
                    act.wait_ge(gate_done, GATES0[k] + n_gates(s) * g + m + 1)
                    gate(4 * q + gt, gates[:, q, gt, 0:n], func_of(gt),
                         lstm_bias[:, 4 * (p - 1) + gt:4 * (p - 1) + gt + 1], n,
                         o_ready if gt == O_ else ifg_ready)
                    if gt == G_ and prev:
                        tanh_cell(*prev)
            tanh_cell(*lstm_slots(act, slot))

            def aggregate(i, first, last):
                if last >= 4:
                    t = i - 4
                    act.wait_ge(lin1_done, t + 1)
                    for k in range(H1):
                        nc.scalar.activation(y[:, k, ds(t, 1), :], ps[:, 2 + k:3 + k, :], ACT.Copy).then_inc(y_ready, 1)
                if first <= 3 <= last:
                    t = i - 3
                    act.wait_ge(agg_done, NT + t + 1)
                    nc.scalar.activation(agg[:], ps[:, 1, :], ACT.Copy).then_inc(agg_ready, 1)
                if first <= 2 <= last:
                    normalise(X[:, ds(i - 2, 1), :], NT + i - 2)
            skewed_loop(act, aggregate, 5)

            act.wait_ge(bn_ready, 1)
            with act.Fori(0, NT) as t:
                for k in range(H1):
                    nc.scalar.activation(y[:, k, ds(t, 1), :], y[:, k, ds(t, 1), :], ACT.Relu,
                                         bias=bn[:, 0, 5, k:k + 1], scale=bn[:, 0, 3, k:k + 1]).then_inc(yr_ready, 1)

            act.wait_ge(bn_ready, 2)

            def scale_out(i, q):
                t = 2 * i + q
                at_least(act, out_done, t - 1)
                nc.scalar.activation(zt[:, q:q + 1, :], z[:, ds(t, 1), :], ACT.Identity,
                                     bias=bn[:, 1, 5, 0:1], scale=bn[:, 1, 3, 0:1]).then_inc(zt_ready, 1)
            scale_out(0, 0)
            scale_out(0, 1)
            with act.Fori(1, NT // 2) as i:
                scale_out(i, 0)
                scale_out(i, 1)

        @block.vector
        def _(dve):
            LN = 4

            def halves(t):
                for b in range(TB):
                    a = nc.vector.bn_stats(st[:, b, :], X[:, ds(t, 1), b * P:(b + 1) * P])
                a.then_inc(ln_steps, 1)

            def variance(n):
                dve.wait_ge(ln_steps, LN * n + 1)
                nc.vector.tensor_tensor(half[:, 0, :], st[:, :, 1], st[:, :, 4], ALU.add)
                nc.vector.tensor_tensor(half[:, 1, :], st[:, :, 1], st[:, :, 4], ALU.subtract)
                nc.vector.tensor_tensor(half[:, 2, :], st[:, :, 2], st[:, :, 5], ALU.add).then_inc(ln_steps, 1)
                dve.wait_ge(ln_steps, LN * n + 2)
                nc.vector.scalar_tensor_tensor(half[:, 3, :], half[:, 1, :], 0.25, half[:, 1, :], ALU.mult, ALU.mult)
                nc.vector.tensor_scalar(half[:, 4, :], half[:, 2, :], 1.0 / P, EPS, ALU.mult, ALU.add
                                        ).then_inc(ln_steps, 1)

            def hand_over(n):
                dve.wait_ge(ln_steps, LN * n + 3)
                at_least(dve, ln_ready, n)
                nc.vector.tensor_scalar(neg_mean[:], half[:, 0, :], -0.5, None, ALU.mult).then_inc(ln_steps, 1)
                nc.vector.tensor_tensor(var_eps[:], half[:, 3, :], half[:, 4, :], ALU.add).then_inc(ln_stats, 1)

            def normalise(t):
                dve.wait_ge(ln_ready, t + 1)
                at_least(dve, f_ready, t)
                for b in range(TB):
                    a = nc.vector.tensor_scalar(xn[:, :, b * P:(b + 1) * P], X[:, ds(t, 1), b * P:(b + 1) * P],
                                                rstd[:, b:b + 1], shift[:, b:b + 1], ALU.mult, ALU.add)
                a.then_inc(xn_ready, 1)

            dve.wait_ge(x_ready, 1)
            halves(0)
            variance(0)
            hand_over(0)
            dve.wait_ge(x_ready, 3)
            halves(1)
            variance(1)
            normalise(0)
            hand_over(1)
            dve.wait_ge(graph_loaded, 32)
            dve.wait_ge(ident_ready, 2)
            for k in range(2):
                a = nc.vector.tensor_tensor(norm[:, k, :], adj_sb[:, k, :], ident[:], ALU.add)
            a.then_inc(norm_steps, 1)
            dve.wait_ge(norm_steps, 1)
            nc.vector.tensor_tensor(ahatT[:], norm[:, 0, :], ident[:], ALU.mult).then_inc(norm_steps, 1)
            nc.vector.reduce_sum(deg3[:, 0:2], norm[:], AX).then_inc(norm_steps, 1)
            dve.wait_ge(norm_steps, 3)
            nc.vector.reduce_sum(deg3[:, 2:3], ahatT[:], AX).then_inc(norm_steps, 1)
            dve.wait_ge(norm_steps, 4)
            nc.vector.tensor_tensor(deg3[:, 3:4], deg3[:, 0:1], deg3[:, 1:2], ALU.add).then_inc(norm_steps, 1)
            dve.wait_ge(norm_steps, 5)
            nc.vector.tensor_tensor(deg3[:, 3:4], deg3[:, 3:4], deg3[:, 2:3], ALU.subtract).then_inc(deg_ready, 1)
            dve.wait_ge(row_bias_done, 1)
            nc.vector.tensor_copy(row_bias[:], ps[:, 7, 0:P]).then_inc(row_bias_ready, 1)
            dve.wait_ge(dinv_ready, 1)
            nc.vector.tensor_scalar(norm[:, 0, :], norm[:, 0, :], dinv[:, 0:1], None, ALU.mult).then_inc(scaled_ready, 1)
            dve.wait_ge(scaledT_done, 1)
            nc.vector.tensor_scalar(ahatT[:], ps[:, 6, 0:P], dinv[:, 0:1], None, ALU.mult).then_inc(ahatT_ready, 1)
            dve.wait_ge(row_bias_ready, 1)

            def convolutions(i, first, last):
                if first == 0 and not (isinstance(i, int) and i + 2 >= NT):
                    halves(i + 2)
                    variance(i + 2)
                if isinstance(i, int) and i == 3:
                    dve.wait_ge(lstm_loaded, 32)
                    nc.vector.tensor_tensor(lstm_bias[:], lstm_b_sb[:, 0, :], lstm_b_sb[:, 1, :], ALU.add
                                            ).then_inc(bias_ready, 1)
                if last >= 5:
                    t = i - 5
                    dve.wait_ge(tanh_ready, t + 1)
                    dve.wait_ge(o_ready, t + 1)
                    at_least(dve, hid_lo_ready, t)
                    nc.vector.tensor_tensor(hid1, gates[:, 1, O_, :], tanh1, ALU.mult).then_inc(hid_ready, 1)
                if first == 0 and not (isinstance(i, int) and i + 3 >= NT):
                    dve.wait_ge(x_ready, i + 4)
                if first == 0 and not (isinstance(i, int) and i + 1 >= NT):
                    normalise(i + 1)
                if first == 0 and not (isinstance(i, int) and i + 2 >= NT):
                    hand_over(i + 2)
                if first <= 2 <= last:
                    t = i - 2
                    dve.wait_ge(u2_done, t + 1)
                    nc.vector.tensor_tensor(u2[:], ps[:, 2, :].rearrange("p (b h) -> p b h", b=TB),
                                            gcn_b_sb[:, 1:2, :].to_broadcast([P, TB, P]),
                                            ALU.add).then_inc(u2_ready, 1)
                if first <= 3 <= last:
                    t = i - 3
                    dve.wait_ge(h0_hi_ready, t + 1)
                    nc.vector.scalar_tensor_tensor(h0_lo, ps[:, 3, :], 0.0, h0_hi.bitcast(f32),
                                                   ALU.max, ALU.subtract).then_inc(h0_ready, 1)
                if first <= 1 <= last:
                    t = i - 1
                    dve.wait_ge(conv1_done, t + 1)
                    nc.vector.tensor_tensor(pre1[:], ps[:, 1, :].rearrange("p (b t) -> p b t", b=TB),
                                            row_bias[:, None, :].to_broadcast([P, TB, P]),
                                            ALU.add).then_inc(pre1_ready, 1)
            for i in range(6):
                convolutions(i, 0, i)
            with dve.Fori(6, NT - 3) as i:
                convolutions(i, 0, 5)
            for i in range(NT - 3, NT + 5):
                convolutions(i, max(0, i - NT + 1), 5)

            def hidden(k, i, q):
                p, s = STEPS[k]
                n, g = GB * windows(p), 2 * i + q
                job = NT + NG * k + g
                dve.wait_ge(o_ready, job + 1)
                dve.wait_ge(tanh_ready, job + 1)
                nc.vector.tensor_tensor(gates[:, q, O_, 0:n], gates[:, q, O_, 0:n], gates[:, q, G_, 0:n],
                                        ALU.mult).then_inc(hid_ready, 1)
                dve.wait_ge(hid_ready, job + 1)
                if s < p - 1:
                    nc.vector.tensor_copy(rec_hi[:, ds(g, 1), 0:n], gates[:, q, O_:O_ + 1, 0:n]
                                          ).then_inc(hid_hi_ready, 1)
                else:
                    nc.vector.tensor_copy(positions(h_hi, g, p, s),
                                          gates[:, q, O_, 0:n].rearrange("p (b w) -> p b w", b=GB)
                                          ).then_inc(hid_hi_ready, 1)

            def slot(k, i, q, prev):
                p, s = STEPS[k]
                n, g = GB * windows(p), 2 * i + q
                c_at = c[:, ds(g, 1), 0:n]
                if prev:
                    hidden(*prev)
                if s == 0:
                    dve.wait_ge(ifg_ready, IFG0[k] + 2 * g + 2)
                    nc.vector.tensor_tensor(c_at, gates[:, q, I_:I_ + 1, 0:n], gates[:, q, G_:G_ + 1, 0:n],
                                            ALU.mult).then_inc(c_ready, 1)
                else:
                    dve.wait_ge(ifg_ready, IFG0[k] + 3 * g + 3)
                    nc.vector.tensor_tensor(gates[:, q, F_:F_ + 1, 0:n], gates[:, q, F_:F_ + 1, 0:n], c_at,
                                            ALU.mult).then_inc(fc_ready, 1)
                    dve.wait_ge(fc_ready, FULL0[k] + g + 1)
                    dve.wait_ge(ig_ready, FULL0[k] + g + 1)
                    nc.vector.tensor_tensor(c_at, gates[:, q, F_:F_ + 1, 0:n], gates[:, q, I_:I_ + 1, 0:n],
                                            ALU.add).then_inc(c_ready, 1)
            hidden(*lstm_slots(dve, slot))

            def aggregate(i, first, last):
                if last >= 4:
                    dve.wait_ge(y_ready, H1 * (i - 4) + H1)
                if first == 0:
                    dve.wait_ge(back_done, i + 1)
                    nc.vector.tensor_tensor(X[:, ds(i, 1), :], ps[:, 0:1, :], X[:, ds(i, 1), :],
                                            ALU.add).then_inc(x_added, 1)
                if last >= 4:
                    t = i - 4
                    for k in range(H1):
                        nc.vector.bn_stats(st1[:, k, ds(t, 1), :], y[:, k, ds(t, 1), :]).then_inc(y_stats, 1)
                if first == 0:
                    dve.wait_ge(x_added, i + 1)
                if first <= 1 <= last:
                    variance(NT + i - 1)
                    hand_over(NT + i - 1)
                if first == 0:
                    halves(i)
            skewed_loop(dve, aggregate, 5)

            def batchnorm(b, width, vec, mean_var, steps):
                w = slice(0, width)
                nc.vector.tensor_tensor(bn[:, b, 1, w], mean_var[:, :, 0], vec[:, 0, :], ALU.add).then_inc(bn_steps, 1)
                nc.vector.tensor_scalar(bn[:, b, 0, w], mean_var[:, :, 1], EPS, None, ALU.add).then_inc(bn_var, 1)
                dve.wait_ge(bn_steps, steps + 1)
                nc.vector.tensor_tensor(bn[:, b, 4, w], vec[:, 0, :], bn[:, b, 1, w], ALU.subtract
                                        ).then_inc(bn_steps, 1)
                dve.wait_ge(bn_rstd, b + 1)
                nc.vector.tensor_tensor(bn[:, b, 3, w], bn[:, b, 2, w], vec[:, 1, :], ALU.mult).then_inc(bn_steps, 1)
                dve.wait_ge(bn_steps, steps + 3)
                nc.vector.tensor_tensor(bn[:, b, 1, w], bn[:, b, 4, w], bn[:, b, 3, w], ALU.mult).then_inc(bn_steps, 1)
                dve.wait_ge(bn_steps, steps + 4)
                nc.vector.tensor_tensor(bn[:, b, 5, w], bn[:, b, 1, w], vec[:, 2, :], ALU.add).then_inc(bn_ready, 1)

            dve.wait_ge(lin_loaded, 64)
            dve.wait_ge(y_stats, H1 * NT)
            for k in range(H1):
                a = nc.vector.bn_aggr(mv1[:, k, :], st1[:, k, :, :].rearrange("p t s -> p (t s)"))
            a.then_inc(bn_steps, 1)
            dve.wait_ge(bn_steps, 1)
            batchnorm(0, H1, vec1_sb, mv1, 1)

            with dve.Fori(0, NT // 2) as i:
                for q in range(2):
                    t = 2 * i + q
                    dve.wait_ge(lin2_done, t + 1)
                    nc.vector.tensor_copy(z[:, ds(t, 1), :], ps[:, 4 + q:5 + q, :]).then_inc(z_ready, 1)
                    nc.vector.bn_stats(st2[:, ds(t, 1), :], ps[:, 4 + q:5 + q, :]).then_inc(z_stats, 1)
            dve.wait_ge(z_stats, NT)
            nc.vector.bn_aggr(mv2[:, 0, :], st2[:, :, :].rearrange("p t s -> p (t s)")).then_inc(bn_steps, 1)
            dve.wait_ge(bn_steps, 6)
            batchnorm(1, 1, vec2_sb, mv2, 6)

            with dve.Fori(0, NT // 2) as i:
                for q in range(2):
                    t = 2 * i + q
                    dve.wait_ge(out_done, t + 1)
                    nc.vector.tensor_tensor(X[:, ds(t, 1), :], ps[:, 6 + q:7 + q, :], X[:, ds(t, 1), :],
                                            ALU.add).then_inc(out_ready, 1)

        @block.tensor
        def _(pe):
            adjT_mov = adj_sb[:, 1, :]

            pe.wait_ge(graph_loaded, 32)
            nc.tensor.matmul(ps[:, 7, 0:P], gcn_b_sb[:, 0, :], adjT_mov, start=True, stop=True).then_inc(row_bias_done, 1)
            pe.wait_ge(ident_ready, 2)
            pe.wait_ge(scaled_ready, 1)
            nc.tensor.transpose(ps[:, 6, 0:P], norm[:, 0, :], ident[:]).then_inc(scaledT_done, 1)
            pe.wait_ge(ahatT_ready, 1)
            pe.wait_ge(row_bias_ready, 1)

            def data_times(bank, data, moving, done):
                for b in range(TB):
                    m = nc.tensor.matmul(ps[:, bank, b * P:(b + 1) * P], data[:, b, :], moving, start=True, stop=True)
                m.then_inc(done, 1)

            def split_product(out_at, m, gt, hi, lo, start, stop):
                w = slice(gt * P, (gt + 1) * P)
                nc.tensor.matmul(out_at, w_hi[:, m, w], hi, start=start, stop=False)
                nc.tensor.matmul(out_at, w_hi[:, m, w], lo, start=False, stop=False)
                return nc.tensor.matmul(out_at, w_lo[:, m, w], hi, start=False, stop=stop)

            def convolutions(i, first, last):
                if last >= 4:
                    t = i - 4
                    if isinstance(i, int) and i == 4:
                        pe.wait_ge(w_ready, 1)
                    pe.wait_ge(h0_ready, t + 1)
                    at_least(pe, o_ready, t)
                    for k, gt in enumerate([I_, G_, O_]):
                        split_product(ps[:, 4 + k, :], 0, gt, h0_hi, h0_lo, True, True).then_inc(gate_done, 1)
                if first <= 3 <= last:
                    pe.wait_ge(u2_ready, i - 3 + 1)
                    data_times(3, u2, adjT_mov, conv2_done)
                if first <= 2 <= last:
                    pe.wait_ge(h1_ready, i - 2 + 1)
                    data_times(2, h1, gcn_w_sb[:, 1, :], u2_done)
                if first <= 1 <= last:
                    pe.wait_ge(agg_ready, i - 1 + 1)
                    nc.tensor.matmul(ps[:, 1, :], gcn_w_sb[:, 0, :], agg[:], start=True, stop=True
                                     ).then_inc(conv1_done, 1)
                if first == 0:
                    pe.wait_ge(f_ready, i + 1)
                    data_times(0, f_in, adjT_mov, agg_done)
            skewed_loop(pe, convolutions, 5)

            pe.wait_ge(w_ready, 7)
            for k, (p, s) in enumerate(STEPS):
                n = GB * windows(p)
                m_ih = 2 * p - 3
                with pe.Fori(0, NG // 2) as i:
                    for q in range(2):
                        g = 2 * i + q
                        if k == 0:
                            pe.wait_ge(hid_lo_ready, 2 * g + 2)
                        else:
                            pe.wait_ge(hid_lo_ready, NT + NG * (k - 1) + g + 1)
                        pe.wait_ge(o_ready, NT + NG * k + g - 1)
                        for gt in gate_order(s):
                            bank = ps[:, 4 * q + gt, 0:n]
                            a = split_product(bank, m_ih, gt, positions(h_hi, g, p, s), positions(h_lo, g, p, s),
                                              True, s == 0)
                            if s > 0:
                                a = split_product(bank, m_ih + 1, gt, rec_hi[:, ds(g, 1), 0:n],
                                                  rec_lo[:, ds(g, 1), 0:n], False, True)
                            a.then_inc(gate_done, 1)

            pe.wait_ge(lin_loaded, 64)
            pe.wait_ge(o_ready, JOBS)

            def aggregate(i, first, last):
                if last >= 4:
                    t = i - 4
                    pe.wait_ge(agg_ready, NT + t + 1)
                    at_least(pe, y_ready, H1 * t)
                    for k in range(H1):
                        m = nc.tensor.matmul(ps[:, 2 + k, :], lin1_sb[:, k * P:(k + 1) * P], agg[:],
                                             start=True, stop=True)
                    m.then_inc(lin1_done, 1)
                if first <= 3 <= last:
                    pe.wait_ge(f_ready, NT + i - 3 + 1)
                    data_times(1, f_in, ahatT[:], agg_done)
                if first == 0:
                    pe.wait_ge(hsum_ready, i + 1)
                    at_least(pe, x_added, i)
                    for b in range(TB):
                        m = nc.tensor.transpose(ps[:, 0, b * P:(b + 1) * P], hsum[:, b, :], ident[:])
                    m.then_inc(back_done, 1)
            skewed_loop(pe, aggregate, 5)

            def second_linear(i, q):
                t = 2 * i + q
                pe.wait_ge(yr_ready, H1 * t + H1)
                at_least(pe, z_stats, t - 1)
                for k in range(H1):
                    m = nc.tensor.matmul(ps[:, 4 + q:5 + q, :], lin2_sb[:, k, :], y[:, k, ds(t, 1), :],
                                         start=(k == 0), stop=(k == H1 - 1))
                m.then_inc(lin2_done, 1)
            second_linear(0, 0)
            second_linear(0, 1)
            with pe.Fori(1, NT // 2) as i:
                second_linear(i, 0)
                second_linear(i, 1)

            def turn_out(i, q):
                t = 2 * i + q
                pe.wait_ge(zt_ready, t + 1)
                at_least(pe, out_ready, t - 1)
                for b in range(TB):
                    m = nc.tensor.transpose(ps[:, 6 + q, b * P:(b + 1) * P], zt[:, q, b * P:(b + 1) * P], ident[:])
                m.then_inc(out_done, 1)
            turn_out(0, 0)
            turn_out(0, 1)
            with pe.Fori(1, NT // 2) as i:
                turn_out(i, 0)
                turn_out(i, 1)


def kernel(**inputs):
    import numpy as np
    import concourse.bacc as bacc
    from concourse.bass_utils import run_bass_kernel_spmd

    def a(name):
        return np.asarray(inputs[name])

    wih, whh = a("L0_gnn_Wih"), a("L0_gnn_Whh")
    order = [(wih, 0)] + [(w, p) for p in range(1, SKIPS) for w in (wih, whh)]
    arrays = {
        "x": a("x").transpose(1, 0, 2).reshape(P, NT, TC),
        "graph": np.stack([a("adj"), a("adj").T, a("L0_gnn_Wg0"), a("L0_gnn_Wg1")], 1),
        "gcn_b": np.stack([a("L0_gnn_bg0"), a("L0_gnn_bg1")], 0),
        "lstm_w": np.stack([w[p].T for w, p in order], 1),
        "lstm_b": np.stack([a(n).reshape(SKIPS * 4, P).T for n in ("L0_gnn_bih", "L0_gnn_bhh")], 1),
        "lin1_w": a("L1_gnn_W1").T,
        "lin2_w": a("L1_gnn_W2").T.reshape(H1, P, P).transpose(1, 0, 2),
        "vec1": np.stack([a(n).reshape(H1, P).T for n in ("L1_gnn_b1", "L1_gnn_g1", "L1_gnn_be1")], 1),
        "vec2": np.stack([a(n).reshape(1, P).T for n in ("L1_gnn_b2", "L1_gnn_g2", "L1_gnn_be2")], 1),
    }
    arrays = {k: np.ascontiguousarray(v) for k, v in arrays.items()}
    nc = bacc.Bacc("TRN2", target_bir_lowering=False, num_devices=1)
    args = [nc.dram_tensor(k, v.shape, mybir.dt.float32, kind="ExternalInput").ap() for k, v in arrays.items()]
    out = nc.dram_tensor("out", (P, NT, TC), mybir.dt.float32, kind="ExternalOutput").ap()
    gnn_kernel(nc, *args, out)
    r = run_bass_kernel_spmd(nc, [arrays], core_ids=[0]).results[0]["out"]
    return np.ascontiguousarray(r.reshape(P, NB, P).transpose(1, 0, 2))
```

```python
import concourse.bass as bass
from concourse import mybir
from collections import namedtuple
from contextlib import ExitStack

P = 128
NB = 64
TB = 4
NT = NB // TB
TC = TB * P
GB = 8
NG = NB // GB
SKIPS = 4
EPS = 1e-5
I_, F_, G_, O_ = range(4)
H1 = 2

STAGES = [(p, s) for p in range(2, SKIPS + 1) for s in range(p)]
LAST = len(STAGES) - 1

Job = namedtuple("Job", "k g q number gates ifg full")


def n_gates(k):
    return 3 if STAGES[k][1] == 0 else 4


def stage_runs():
    def pairs(n, *body):
        return [(list(body), n)]
    p2, p3, p4 = STAGES.index((2, 0)), STAGES.index((3, 0)), STAGES.index((4, 0))
    return (pairs(2, (p2, 0, 2), (p2, 1, 2))
            + pairs(NG - 4, (p2, 4, 1), (p2 + 1, 0, 1))
            + pairs(4, (p3, 0, 1), (p2 + 1, NG - 4, 1))
            + pairs(NG - 4, (p3, 4, 1), (p3 + 1, 0, 1))
            + pairs(2, (p3 + 1, NG - 4, 2), (p3 + 1, NG - 3, 2))
            + pairs(1, (p3 + 2, 0, 0), (p3 + 2, 1, 0))
            + pairs(NG - 2, (p3 + 2, 2, 1), (p4, 0, 1))
            + pairs(2, (p4 + 1, 0, 1), (p4, NG - 2, 1))
            + pairs(NG // 2 - 1, (p4 + 1, 2, 2), (p4 + 1, 3, 2))
            + pairs(NG // 2, (p4 + 2, 0, 2), (p4 + 2, 1, 2))
            + pairs(1, (LAST, 0, 0), (LAST, 1, 0)))


def job_at(body, start, i, q):
    def counts(k):
        return (1, n_gates(k), n_gates(k) - 1, n_gates(k) - 3)
    each = [counts(k) for k, _, _ in body]
    at = [a + sum(e) * i + (e[0] if q else 0) for a, e in zip(start, zip(*each))]
    k, g0, dg = body[q]
    return Job(k, g0 + dg * i if dg else g0, q, *at)


def run_starts():
    at, out = [NT, 3 * NT, 2 * NT, 0], []
    for body, n in stage_runs():
        out.append((body, n, at))
        end = job_at(body, at, n, 0)
        at = [end.number, end.gates, end.ifg, end.full]
    return out, at


RUNS, LAST_START = run_starts()
NUMBER = {(j.k, j.g): j.number for body, n, at in RUNS for i in range(n) for q in range(2)
          for j in [job_at(body, at, i, q)]}


def first_job():
    body, _, start = RUNS[0]
    return job_at(body, start, 0, 0)


def last_job(g):
    return Job(LAST, g, 0, *(a + e * (g - 2) for a, e in zip(LAST_START, (1, 4, 3, 1))))


def jobs_needed(job, body, n):
    if job.k == 0:
        return 2 * job.g + 2
    if isinstance(job.g, int):
        return NUMBER[job.k - 1, job.g] + 1
    k, g0, dg = body[job.q]
    back = min(NUMBER[k, g] - NUMBER[k - 1, g] for g in (g0 + dg * i for i in range(1, n)))
    return job.number - back + 1


def at_least(engine, sem, value):
    if isinstance(value, int) and value < 1:
        return
    engine.wait_ge(sem, value)


def gnn_kernel(nc, x, graph, gcn_b, lstm_w, lstm_b, lin1_w, lin2_w, vec1, vec2, out):
    f32, f32r = mybir.dt.float32, mybir.dt.float32r
    ACT, ALU, AX = mybir.ActivationFunctionType, mybir.AluOpType, mybir.AxisListType.X
    ds = bass.ds

    with ExitStack() as ctx:
        def sb(name, shape, dt=f32):
            return ctx.enter_context(nc.sbuf_tensor(name, shape, dt))

        def sem(name):
            return ctx.enter_context(nc.semaphore(name))

        HB = NB * P * 4
        base = (nc.sbuf_usable_end - 2 * HB) // 32 * 32
        h_hi = nc.alloc_sbuf_tensor_at("h_hi", [P, NB, P], f32r, offset=base)
        h_lo = nc.alloc_sbuf_tensor_at("h_lo", [P, NB, P], f32r, offset=base + HB)
        y = nc.alloc_sbuf_tensor_at("y", [P, H1, NT, TC], f32, offset=base)
        z = y[:, 0]
        X = sb("X", [P, NT, TC])
        rec_hi = sb("rec_hi", [P, NG, GB * 64], f32r)
        rec_lo = sb("rec_lo", [P, NG, GB * 64], f32r)
        c = sb("c", [P, NG, GB * 64])
        w_hi = sb("w_hi", [P, 7, 4 * P], f32r)
        w_lo = sb("w_lo", [P, 7, 4 * P], f32r)
        w_raw = c[:, :, :].rearrange("p g n -> p (g n)")[:, 0:7 * 4 * P].rearrange("p (m n) -> p m n", m=7)
        gates = sb("gates", [P, 2, 4, TC])
        cell1, tanh1, hid1 = gates[:, 1, F_, :], gates[:, 0, F_, :], c[:, 3, :]
        f_in = sb("f_in", [P, TB, P])
        agg = sb("agg", [P, TC])
        pre1 = sb("pre1", [P, TB, P])
        h1 = sb("h1", [P, TB, P])
        u2 = sb("u2", [P, TB, P])
        h0_hi = rec_hi[:, NG - 1, :]
        h0_lo = rec_lo[:, NG - 1, :]
        hsum = (pre1, u2)
        agg2 = (agg[:], h1[:, :, :].rearrange("p b t -> p (b t)"))
        xn = c[:, NG - 1:NG, :]
        zt = gates[:, 0]
        graph_sb = sb("graph_sb", [P, 4, P])
        adj_sb, gcn_w_sb = graph_sb[:, 0:2, :], graph_sb[:, 2:4, :]
        norm = sb("norm", [P, 2, P])
        ahatT = sb("ahatT", [P, P])
        ident = sb("ident", [P, P])
        gcn_b_sb = sb("gcn_b_sb", [P, 2, P])
        row_bias = sb("row_bias", [P, P])
        lin1_sb = sb("lin1_sb", [P, H1 * P])
        lin2_sb = sb("lin2_sb", [P, H1, P])
        lstm_b_sb = sb("lstm_b_sb", [P, 2, SKIPS * 4])
        lstm_bias = sb("lstm_bias", [P, SKIPS * 4])
        vec1_sb = sb("vec1_sb", [P, 3, H1])
        vec2_sb = sb("vec2_sb", [P, 3, 1])
        mhalf = sb("mhalf", [P, TB])
        deg3 = sb("deg3", [P, 4])
        dinv = sb("dinv", [P, 1])
        st = sb("st", [P, TB, 6])
        half = sb("half", [P, 5, TB])
        var_eps = sb("var_eps", [P, TB])
        neg_mean = sb("neg_mean", [P, TB])
        rstd = sb("rstd", [P, TB])
        shift = sb("shift", [P, TB])
        st1 = sb("st1", [P, H1, NT, 6])
        st2 = sb("st2", [P, NT, 6])
        bn_mv = sb("bn_mv", [P, H1 + 1, 2])
        bn_sum, bn_diff, bn_gdiff, bn_var_eps, bn_rs, bn_scale, bn_shift = (
            sb(f"bn_{k}", [P, H1 + 1]) for k in ("sum", "diff", "gdiff", "var_eps", "rs", "scale", "shift"))
        assert nc.sbuf_base <= base, (nc.sbuf_base, base)
        ps = ctx.enter_context(nc.psum_tensor("ps", [P, 8, TC], f32))

        graph_loaded = sem("graph_loaded")
        x_dma = [sem(f"x_dma{k}") for k in range(7)]
        x_ready = sem("x_ready")
        lstm_loaded = sem("lstm_loaded")
        lin_loaded = sem("lin_loaded")
        ident_ready = sem("ident_ready")
        mhalf_ready = sem("mhalf_ready")
        norm_steps = sem("norm_steps")
        deg_ready = sem("deg_ready")
        dinv_ready = sem("dinv_ready")
        scaled_ready = sem("scaled_ready")
        scaledT_done = sem("scaledT_done")
        ahatT_ready = sem("ahatT_ready")
        row_bias_done = sem("row_bias_done")
        row_bias_ready = sem("row_bias_ready")
        bias_ready = sem("bias_ready")
        w_hi_ready = sem("w_hi_ready")
        w_ready = sem("w_ready")
        ln_steps = sem("ln_steps")
        ln_stats = sem("ln_stats")
        rstd_done = sem("rstd_done")
        ln_ready = sem("ln_ready")
        xn_ready = sem("xn_ready")
        f_ready = sem("f_ready")
        agg_done = sem("agg_done")
        agg_ready = sem("agg_ready")
        conv1_done = sem("conv1_done")
        pre1_ready = sem("pre1_ready")
        h1_ready = sem("h1_ready")
        u2_done = sem("u2_done")
        u2_ready = sem("u2_ready")
        conv2_done = sem("conv2_done")
        h0_hi_ready = sem("h0_hi_ready")
        h0_ready = sem("h0_ready")
        gate_done = sem("gate_done")
        ifg_ready = sem("ifg_ready")
        o_ready = sem("o_ready")
        ig_ready = sem("ig_ready")
        fc_ready = sem("fc_ready")
        c_ready = sem("c_ready")
        tanh_ready = sem("tanh_ready")
        hid_ready = sem("hid_ready")
        hid_hi_ready = sem("hid_hi_ready")
        hid_lo_ready = sem("hid_lo_ready")
        hsum_ready = sem("hsum_ready")
        back_done = sem("back_done")
        x_added = sem("x_added")
        lin1_done = sem("lin1_done")
        y_ready = sem("y_ready")
        y_stats = sem("y_stats")
        bn_steps = sem("bn_steps")
        bn_var = sem("bn_var")
        bn_rstd = sem("bn_rstd")
        bn_ready = sem("bn_ready")
        yr_ready = sem("yr_ready")
        lin2_done = sem("lin2_done")
        z_ready = sem("z_ready")
        z_stats = sem("z_stats")
        zt_ready = sem("zt_ready")
        out_done = sem("out_done")
        out_ready = sem("out_ready")
        stored = sem("stored")

        X_CHUNKS = [1, 1, 2, 2, 2, 4, 4]

        def windows(p):
            return P // p

        def gate_order(s):
            return [I_, G_, O_] if s == 0 else [I_, G_, F_, O_]

        def positions(h, g, p, s, nb=GB):
            nw = windows(p)
            return h[:, ds(nb * g, nb), s:s + p * (nw - 1) + 1:p]

        def skewed_loop(engine, body, n_stages):
            for i in range(n_stages):
                body(i, 0, i)
            with engine.Fori(n_stages, NT) as i:
                body(i, 0, n_stages - 1)
            for i in range(NT, NT + n_stages - 1):
                body(i, i - NT + 1, n_stages - 1)

        def lstm_slots(engine, slot):
            prev = None
            for body, n, start in RUNS:
                def pair(i, prev):
                    for q in range(2):
                        job = job_at(body, start, i, q)
                        slot(job, prev, (body, n))
                        prev = job
                pair(0, prev)
                if n > 1:
                    with engine.Fori(1, n) as i:
                        pair(i, job_at(body, start, i - 1, 1))
                prev = job_at(body, start, n - 1, 1)
            return prev

        def last_buffers(job):
            return job.number - 1 if isinstance(job.g, int) and job.g == 2 else job.number

        def closing_loop(early, tile, engine, n_stages):
            def iteration(i):
                early(last_job(i))
                for u in range(2):
                    n = 2 * i - 4 + u
                    tile(n, u, 0, min(n, n_stages - 1) if isinstance(n, int) else n_stages - 1, last_job(i))
            peeled = 2 + (n_stages + 1) // 2
            for i in range(2, peeled):
                iteration(i)
            with engine.Fori(peeled, NG) as i:
                iteration(i)
            for n in range(2 * NG - 4, NT + n_stages - 1):
                tile(n, n % 2, max(0, n - NT + 1), n_stages - 1, None)

        block = ctx.enter_context(nc.Block())

        @block.sync
        def _(sp):
            t = 0
            for k, n in enumerate(X_CHUNKS):
                sp.dma_start(X[:, t:t + n, :], x[:, t:t + n, :]).then_inc(x_dma[k], 16)
                t += n
                if k == 0:
                    sp.dma_start(graph_sb[:], graph).then_inc(graph_loaded, 16)
                    sp.dma_start(gcn_b_sb[:], gcn_b.partition_broadcast(P)).then_inc(graph_loaded, 16)
                if k == 3:
                    sp.dma_start(w_raw, lstm_w).then_inc(lstm_loaded, 16)
                    sp.dma_start(lstm_b_sb[:], lstm_b).then_inc(lstm_loaded, 16)
            sp.dma_start(lin1_sb[:], lin1_w).then_inc(lin_loaded, 16)
            sp.dma_start(lin2_sb[:], lin2_w).then_inc(lin_loaded, 16)
            sp.dma_start(vec1_sb[:], vec1).then_inc(lin_loaded, 16)
            sp.dma_start(vec2_sb[:], vec2).then_inc(lin_loaded, 16)
            for k, n in enumerate(X_CHUNKS):
                sp.wait_ge(x_dma[k], 16)
                sp.sem_inc(x_ready, n)
            for t in range(4):
                sp.wait_ge(out_ready, t + 1)
                sp.dma_start(out[:, t:t + 1, :], X[:, t:t + 1, :]).then_inc(stored, 16)
            with sp.Fori(2, NT // 2) as i:
                sp.wait_ge(out_ready, 2 * i + 2)
                sp.dma_start(out[:, ds(2 * i, 2), :], X[:, ds(2 * i, 2), :]).then_inc(stored, 16)
            sp.wait_ge(stored, 16 * (NT // 2 + 2))

        @block.gpsimd
        def _(pool):
            nc.gpsimd.memset(mhalf[:], -0.5).then_inc(mhalf_ready, 1)
            nc.gpsimd.memset(ident[:], 0.0).then_inc(ident_ready, 1)
            pool.wait_ge(ident_ready, 1)
            nc.gpsimd.affine_select(out=ident[:], in_=ident[:], compare_op=ALU.not_equal, fill=1.0, base=0,
                                    pattern=[[-1, P]], channel_multiplier=1).then_inc(ident_ready, 1)
            pool.wait_ge(mhalf_ready, 1)

            def layernorm_rstd(n, used):
                pool.wait_ge(ln_stats, n + 1)
                at_least(pool, used, n)
                nc.gpsimd.tensor_tensor(rstd[:], var_eps[:], mhalf[:], ALU.pow).then_inc(rstd_done, 1)
                pool.wait_ge(rstd_done, n + 1)
                nc.gpsimd.tensor_tensor(shift[:], neg_mean[:], rstd[:], ALU.mult).then_inc(ln_ready, 1)

            def weights_lo(m):
                pool.wait_ge(w_hi_ready, m + 1)
                nc.gpsimd.tensor_tensor(w_lo[:, m, :], w_raw[:, m, :], w_hi[:, m, :].bitcast(f32),
                                        ALU.subtract).then_inc(w_ready, 1)

            layernorm_rstd(0, xn_ready)

            def convolutions(i, first, last):
                if first == 0 and not (isinstance(i, int) and i + 1 >= NT):
                    layernorm_rstd(i + 1, xn_ready)
                if isinstance(i, int) and i == 2:
                    pool.wait_ge(deg_ready, 1)
                    nc.gpsimd.tensor_tensor(dinv[:], deg3[:, 3:4], mhalf[:, 0:1], ALU.pow).then_inc(dinv_ready, 1)
                if first <= 4 <= last:
                    t = i - 4
                    pool.wait_ge(ifg_ready, 2 * (t + 1))
                    at_least(pool, tanh_ready, t)
                    nc.gpsimd.tensor_tensor(cell1, gates[:, 1, I_, :], gates[:, 1, G_, :],
                                            ALU.mult).then_inc(c_ready, 1)
                if last >= 5:
                    t = i - 5
                    pool.wait_ge(hid_hi_ready, t + 1)
                    nc.gpsimd.tensor_tensor(h_lo[:, ds(TB * t, TB), :],
                                            hid1.rearrange("p (b t) -> p b t", b=TB),
                                            h_hi[:, ds(TB * t, TB), :].bitcast(f32),
                                            ALU.subtract).then_inc(hid_lo_ready, 1)
                if isinstance(i, int) and 2 <= i <= 5:
                    for m in range(2 * i - 4, min(2 * i - 2, 7)):
                        weights_lo(m)
            for i in range(6):
                convolutions(i, 0, i)
            with pool.Fori(6, NT - 1) as i:
                convolutions(i, 0, 5)
            for i in range(NT - 1, NT + 5):
                convolutions(i, max(0, i - NT + 1), 5)

            def low_part(job):
                (p, s), g, q = STAGES[job.k], job.g, job.q
                n = GB * windows(p)
                pool.wait_ge(hid_hi_ready, job.number + 1)
                if s < p - 1:
                    lo_at, hi_at = rec_lo[:, ds(g, 1), 0:n], rec_hi[:, ds(g, 1), 0:n]
                    hid = gates[:, q, O_:O_ + 1, 0:n]
                else:
                    lo_at, hi_at = positions(h_lo, g, p, s), positions(h_hi, g, p, s)
                    hid = gates[:, q, O_, 0:n].rearrange("p (b w) -> p b w", b=GB)
                nc.gpsimd.tensor_tensor(lo_at, hid, hi_at.bitcast(f32), ALU.subtract).then_inc(hid_lo_ready, 1)
                if job.k == LAST:
                    pool.wait_ge(hid_lo_ready, job.number + 1)

            def input_gate(job):
                n, q = GB * windows(STAGES[job.k][0]), job.q
                pool.wait_ge(ifg_ready, job.ifg + 2)
                nc.gpsimd.tensor_tensor(gates[:, q, I_, 0:n], gates[:, q, I_, 0:n],
                                        gates[:, q, G_, 0:n], ALU.mult).then_inc(ig_ready, 1)

            def slot(job, prev, run):
                if STAGES[job.k][1] > 0:
                    input_gate(job)
                if prev:
                    low_part(prev)
            prev = lstm_slots(pool, slot)

            def gather(t, u):
                nc.gpsimd.tensor_tensor(hsum[u][:], h_hi[:, ds(TB * t, TB), :].bitcast(f32),
                                        h_lo[:, ds(TB * t, TB), :].bitcast(f32), ALU.add).then_inc(hsum_ready, 1)

            def rstd_and_gather(n, u, first, last, job):
                if first == 0 and not (isinstance(n, int) and n + 1 >= NT):
                    at_least(pool, back_done, n)
                    gather(n + 1, 1 - u)
                if isinstance(n, int) and n == 0:
                    low_part(prev)
                if job and u == 1:
                    low_part(job)
                if first <= 1 <= last:
                    layernorm_rstd(NT + n - 1, f_ready)
            gather(0, 0)
            closing_loop(input_gate, rstd_and_gather, pool, 2)

            for j in range(H1 + 1):
                pool.wait_ge(bn_var, j + 1)
                nc.gpsimd.tensor_tensor(bn_rs[:, j:j + 1], bn_var_eps[:, j:j + 1], mhalf[:, 0:1],
                                        ALU.pow).then_inc(bn_rstd, 1)

        @block.scalar
        def _(act):
            def weights_hi(m):
                if m == 0:
                    act.wait_ge(lstm_loaded, 32)
                nc.scalar.activation(w_hi[:, m, :], w_raw[:, m, :], ACT.Copy).then_inc(w_hi_ready, 1)

            def normalise(rows, n):
                act.wait_ge(ln_ready, n + 1)
                act.wait_ge(agg_done, n)
                for b in range(TB):
                    a = nc.scalar.activation(f_in[:, b:b + 1, :], rows[:, :, b * P:(b + 1) * P], ACT.Relu,
                                             bias=shift[:, b:b + 1], scale=rstd[:, b:b + 1])
                a.then_inc(f_ready, 1)

            def gate(k_bank, dst, func, bias, n, done):
                nc.scalar.activation(dst, ps[:, k_bank, 0:n], func, bias=bias).then_inc(done, 1)

            def func_of(g):
                return ACT.Tanh if g == G_ else ACT.Sigmoid

            def relu_in(t):
                act.wait_ge(xn_ready, t + 1)
                at_least(act, agg_done, t)
                nc.scalar.activation(f_in[:], xn.rearrange("p a (b d) -> p (a b) d", b=TB), ACT.Relu
                                     ).then_inc(f_ready, 1)

            def tanh_cell(job):
                n, g, q = GB * windows(STAGES[job.k][0]), job.g, job.q
                act.wait_ge(c_ready, job.number + 1)
                nc.scalar.activation(gates[:, q, G_:G_ + 1, 0:n], c[:, ds(g, 1), 0:n], ACT.Tanh).then_inc(tanh_ready, 1)

            def lstm_gates(job, buffers_used, prev=None):
                (p, s), q = STAGES[job.k], job.q
                n = GB * windows(p)
                for m, gt in enumerate(gate_order(s)):
                    at_least(act, {I_: c_ready, G_: hid_ready, F_: c_ready, O_: hid_lo_ready}[gt], buffers_used)
                    act.wait_ge(gate_done, job.gates + m + 1)
                    gate(4 * q + gt, gates[:, q, gt, 0:n], func_of(gt),
                         lstm_bias[:, 4 * (p - 1) + gt:4 * (p - 1) + gt + 1], n,
                         o_ready if gt == O_ else ifg_ready)
                    if gt == G_ and prev:
                        tanh_cell(prev)

            def convolutions(i, first, last):
                if first <= 2 <= last:
                    act.wait_ge(pre1_ready, i - 2 + 1)
                    nc.scalar.activation(h1[:], pre1[:], ACT.Relu).then_inc(h1_ready, 1)
                if first <= 1 <= last:
                    act.wait_ge(agg_done, i - 1 + 1)
                    nc.scalar.activation(agg[:], ps[:, 0, :], ACT.Copy).then_inc(agg_ready, 1)
                if last >= 5:
                    t = i - 5
                    act.wait_ge(c_ready, t + 1)
                    at_least(act, hid_ready, t)
                    nc.scalar.activation(tanh1, cell1, ACT.Tanh).then_inc(tanh_ready, 1)
                if first == 0:
                    relu_in(i)
                if first <= 4 <= last:
                    t = i - 4
                    if isinstance(i, int) and i == 4:
                        act.wait_ge(bias_ready, 1)
                    for k, g in enumerate([I_, G_, O_]):
                        at_least(act, hid_ready if g == O_ else c_ready, t)
                        act.wait_ge(gate_done, 3 * t + k + 1)
                        gate(4 + k, gates[:, 1, g, :], func_of(g), lstm_bias[:, g:g + 1], TC,
                             o_ready if g == O_ else ifg_ready)
                if first <= 3 <= last:
                    act.wait_ge(conv2_done, i - 3 + 1)
                    nc.scalar.activation(h0_hi, ps[:, 3, :], ACT.Relu).then_inc(h0_hi_ready, 1)
                if isinstance(i, int) and i == NT + 4:
                    lstm_gates(first_job(), 0)
                if last >= 5:
                    t = i - 5
                    act.wait_ge(hid_ready, t + 1)
                    nc.scalar.activation(h_hi[:, ds(TB * t, TB), :], hid1.rearrange("p (b t) -> p b t", b=TB),
                                         ACT.Copy).then_inc(hid_hi_ready, 1)
                if isinstance(i, int) and 2 <= i <= 5:
                    for m in range(2 * i - 4, min(2 * i - 2, 7)):
                        weights_hi(m)
            skewed_loop(act, convolutions, 6)

            def slot(job, prev, run):
                if prev:
                    lstm_gates(job, job.number - 1, prev)
            tanh_cell(lstm_slots(act, slot))

            def aggregate(n, u, first, last, job):
                def copy_y(t, k):
                    act.wait_ge(lin1_done, H1 * t + k + 1)
                    nc.scalar.activation(y[:, k, ds(t, 1), :], ps[:, 6 + k:7 + k, :], ACT.Copy).then_inc(y_ready, 1)
                if last >= 5:
                    copy_y(n - 5, 1)
                if first <= 4 <= last:
                    copy_y(n - 4, 0)
                if first <= 3 <= last:
                    t = n - 3
                    act.wait_ge(agg_done, NT + t + 1)
                    at_least(act, lin1_done, H1 * (t - 1))
                    nc.scalar.activation(agg2[1 - u], ps[:, 5, :], ACT.Copy).then_inc(agg_ready, 1)
                if job and u == 0:
                    tanh_cell(job)
                if first <= 2 <= last:
                    normalise(X[:, ds(n - 2, 1), :], NT + n - 2)
            closing_loop(lambda job: lstm_gates(job, last_buffers(job)), aggregate, act, 6)

            def relu_y(t, k):
                nc.scalar.activation(y[:, k, ds(t, 1), :], y[:, k, ds(t, 1), :], ACT.Relu,
                                     bias=bn_shift[:, k:k + 1], scale=bn_scale[:, k:k + 1]).then_inc(yr_ready, 1)
            for k in range(H1):
                act.wait_ge(bn_ready, k + 1)
                relu_y(0, k)
            with act.Fori(1, NT) as t:
                for k in range(H1):
                    relu_y(t, k)

            act.wait_ge(bn_ready, H1 + 1)
            act.wait_ge(z_ready, NT - 1)

            def scale_out(t, h, n):
                nc.scalar.activation(zt[:, h:h + n, :], z[:, ds(t, n), :], ACT.Identity,
                                     bias=bn_shift[:, H1:H1 + 1], scale=bn_scale[:, H1:H1 + 1]).then_inc(zt_ready, n)
            for t in range(4):
                scale_out(t, t, 1)
            act.wait_ge(z_ready, NT)
            with act.Fori(1, NT // 4) as i:
                for q in range(2):
                    act.wait_ge(out_done, 4 * i + 2 * q - 2)
                    scale_out(4 * i + 2 * q, 2 * q, 2)

        @block.vector
        def _(dve):
            LN = 4

            def halves(t):
                for b in range(TB):
                    a = nc.vector.bn_stats(st[:, b, :], X[:, ds(t, 1), b * P:(b + 1) * P])
                a.then_inc(ln_steps, 1)

            def variance(n):
                dve.wait_ge(ln_steps, LN * n + 1)
                nc.vector.tensor_tensor(half[:, 0, :], st[:, :, 1], st[:, :, 4], ALU.add)
                nc.vector.tensor_tensor(half[:, 1, :], st[:, :, 1], st[:, :, 4], ALU.subtract)
                nc.vector.tensor_tensor(half[:, 2, :], st[:, :, 2], st[:, :, 5], ALU.add).then_inc(ln_steps, 1)
                dve.wait_ge(ln_steps, LN * n + 2)
                nc.vector.scalar_tensor_tensor(half[:, 3, :], half[:, 1, :], 0.25, half[:, 1, :], ALU.mult, ALU.mult)
                nc.vector.tensor_scalar(half[:, 4, :], half[:, 2, :], 1.0 / P, EPS, ALU.mult, ALU.add
                                        ).then_inc(ln_steps, 1)

            def hand_over(n):
                dve.wait_ge(ln_steps, LN * n + 3)
                at_least(dve, ln_ready, n)
                nc.vector.tensor_scalar(neg_mean[:], half[:, 0, :], -0.5, None, ALU.mult).then_inc(ln_steps, 1)
                nc.vector.tensor_tensor(var_eps[:], half[:, 3, :], half[:, 4, :], ALU.add).then_inc(ln_stats, 1)

            def normalise(t):
                dve.wait_ge(ln_ready, t + 1)
                at_least(dve, f_ready, t)
                for b in range(TB):
                    a = nc.vector.tensor_scalar(xn[:, :, b * P:(b + 1) * P], X[:, ds(t, 1), b * P:(b + 1) * P],
                                                rstd[:, b:b + 1], shift[:, b:b + 1], ALU.mult, ALU.add)
                a.then_inc(xn_ready, 1)

            dve.wait_ge(x_dma[0], 16)
            halves(0)
            variance(0)
            hand_over(0)
            dve.wait_ge(x_dma[1], 16)
            halves(1)
            variance(1)
            normalise(0)
            hand_over(1)
            dve.wait_ge(row_bias_done, 1)
            nc.vector.tensor_copy(row_bias[:], ps[:, 7, 0:P]).then_inc(row_bias_ready, 1)
            dve.wait_ge(row_bias_ready, 1)
            dve.wait_ge(x_ready, 3)

            def degrees():
                dve.wait_ge(graph_loaded, 32)
                dve.wait_ge(ident_ready, 2)
                for k in range(2):
                    a = nc.vector.tensor_tensor(norm[:, k, :], adj_sb[:, k, :], ident[:], ALU.add)
                a.then_inc(norm_steps, 1)
                dve.wait_ge(norm_steps, 1)
                nc.vector.tensor_tensor(ahatT[:], norm[:, 0, :], ident[:], ALU.mult).then_inc(norm_steps, 1)
                nc.vector.reduce_sum(deg3[:, 0:2], norm[:], AX).then_inc(norm_steps, 1)
                dve.wait_ge(norm_steps, 3)
                nc.vector.reduce_sum(deg3[:, 2:3], ahatT[:], AX).then_inc(norm_steps, 1)
                dve.wait_ge(norm_steps, 4)
                nc.vector.tensor_tensor(deg3[:, 3:4], deg3[:, 0:1], deg3[:, 1:2], ALU.add).then_inc(norm_steps, 1)
                dve.wait_ge(norm_steps, 5)
                nc.vector.tensor_tensor(deg3[:, 3:4], deg3[:, 3:4], deg3[:, 2:3], ALU.subtract).then_inc(deg_ready, 1)

            def scale_graph(step):
                if step == 0:
                    dve.wait_ge(dinv_ready, 1)
                    nc.vector.tensor_scalar(norm[:, 0, :], norm[:, 0, :], dinv[:, 0:1], None, ALU.mult
                                            ).then_inc(scaled_ready, 1)
                else:
                    dve.wait_ge(scaledT_done, 1)
                    nc.vector.tensor_scalar(ahatT[:], ps[:, 7, 0:P], dinv[:, 0:1], None, ALU.mult
                                            ).then_inc(ahatT_ready, 1)

            def convolutions(i, first, last):
                if first == 0 and not (isinstance(i, int) and i + 2 >= NT):
                    halves(i + 2)
                    variance(i + 2)
                if isinstance(i, int) and i == 5:
                    dve.wait_ge(w_ready, 4)
                if isinstance(i, int) and i == 3:
                    dve.wait_ge(lstm_loaded, 32)
                    nc.vector.tensor_tensor(lstm_bias[:], lstm_b_sb[:, 0, :], lstm_b_sb[:, 1, :], ALU.add
                                            ).then_inc(bias_ready, 1)
                if last >= 5:
                    t = i - 5
                    dve.wait_ge(tanh_ready, t + 1)
                    dve.wait_ge(o_ready, t + 1)
                    at_least(dve, hid_lo_ready, t)
                    nc.vector.tensor_tensor(hid1, gates[:, 1, O_, :], tanh1, ALU.mult).then_inc(hid_ready, 1)
                if first == 0 and not (isinstance(i, int) and i + 3 >= NT):
                    dve.wait_ge(x_ready, i + 4)
                if first == 0 and not (isinstance(i, int) and i + 1 >= NT):
                    normalise(i + 1)
                if first == 0 and not (isinstance(i, int) and i + 2 >= NT):
                    hand_over(i + 2)
                def second_lo():
                    t = i - 3
                    dve.wait_ge(h0_hi_ready, t + 1)
                    nc.vector.scalar_tensor_tensor(h0_lo, ps[:, 3, :], 0.0, h0_hi.bitcast(f32),
                                                   ALU.max, ALU.subtract).then_inc(h0_ready, 1)
                ending = isinstance(i, int) and i >= NT
                if ending and first <= 3 <= last:
                    second_lo()
                if first <= 2 <= last:
                    t = i - 2
                    dve.wait_ge(u2_done, t + 1)
                    nc.vector.tensor_tensor(u2[:], ps[:, 2, :].rearrange("p (b h) -> p b h", b=TB),
                                            gcn_b_sb[:, 1:2, :].to_broadcast([P, TB, P]),
                                            ALU.add).then_inc(u2_ready, 1)
                if not ending and first <= 3 <= last:
                    second_lo()
                if first <= 1 <= last:
                    t = i - 1
                    dve.wait_ge(conv1_done, t + 1)
                    nc.vector.tensor_tensor(pre1[:], ps[:, 1, :].rearrange("p (b t) -> p b t", b=TB),
                                            row_bias[:, None, :].to_broadcast([P, TB, P]),
                                            ALU.add).then_inc(pre1_ready, 1)
                if isinstance(i, int) and 1 <= i <= 4:
                    if i == 1:
                        degrees()
                    elif i == 2:
                        scale_graph(0)
                    elif i == 4:
                        scale_graph(1)
            for i in range(6):
                convolutions(i, 0, i)
            with dve.Fori(6, NT - 3) as i:
                convolutions(i, 0, 5)
            for i in range(NT - 3, NT + 5):
                convolutions(i, max(0, i - NT + 1), 5)

            def hidden(job):
                (p, s), g, q = STAGES[job.k], job.g, job.q
                n = GB * windows(p)
                dve.wait_ge(o_ready, job.number + 1)
                dve.wait_ge(tanh_ready, job.number + 1)
                nc.vector.tensor_tensor(gates[:, q, O_, 0:n], gates[:, q, O_, 0:n], gates[:, q, G_, 0:n],
                                        ALU.mult).then_inc(hid_ready, 1)
                dve.wait_ge(hid_ready, job.number + 1)
                if s < p - 1:
                    nc.vector.tensor_copy(rec_hi[:, ds(g, 1), 0:n], gates[:, q, O_:O_ + 1, 0:n]
                                          ).then_inc(hid_hi_ready, 1)
                else:
                    nc.vector.tensor_copy(positions(h_hi, g, p, s),
                                          gates[:, q, O_, 0:n].rearrange("p (b w) -> p b w", b=GB)
                                          ).then_inc(hid_hi_ready, 1)

            def cell(job):
                (p, s), g, q = STAGES[job.k], job.g, job.q
                n = GB * windows(p)
                c_at = c[:, ds(g, 1), 0:n]
                if s == 0:
                    dve.wait_ge(ifg_ready, job.ifg + 2)
                    nc.vector.tensor_tensor(c_at, gates[:, q, I_:I_ + 1, 0:n], gates[:, q, G_:G_ + 1, 0:n],
                                            ALU.mult).then_inc(c_ready, 1)
                else:
                    dve.wait_ge(ifg_ready, job.ifg + 3)
                    nc.vector.tensor_tensor(gates[:, q, F_:F_ + 1, 0:n], gates[:, q, F_:F_ + 1, 0:n], c_at,
                                            ALU.mult).then_inc(fc_ready, 1)
                    dve.wait_ge(fc_ready, job.full + 1)
                    dve.wait_ge(ig_ready, job.full + 1)
                    nc.vector.tensor_tensor(c_at, gates[:, q, F_:F_ + 1, 0:n], gates[:, q, I_:I_ + 1, 0:n],
                                            ALU.add).then_inc(c_ready, 1)

            def slot(job, prev, run):
                if prev:
                    hidden(prev)
                cell(job)
            hidden(lstm_slots(dve, slot))

            def batchnorm(j, statistics, vec, k):
                at = slice(j, j + 1)
                nc.vector.bn_aggr(bn_mv[:, j, :], statistics.rearrange("p t s -> p (t s)")).then_inc(bn_steps, 1)
                dve.wait_ge(bn_steps, 4 * j + 1)
                nc.vector.tensor_scalar(bn_var_eps[:, at], bn_mv[:, j, 1:2], EPS, None, ALU.add).then_inc(bn_var, 1)
                nc.vector.tensor_tensor(bn_sum[:, at], bn_mv[:, j, 0:1], vec[:, 0, k:k + 1], ALU.add
                                        ).then_inc(bn_steps, 1)
                dve.wait_ge(bn_steps, 4 * j + 2)
                nc.vector.tensor_tensor(bn_diff[:, at], vec[:, 0, k:k + 1], bn_sum[:, at], ALU.subtract
                                        ).then_inc(bn_steps, 1)
                dve.wait_ge(bn_steps, 4 * j + 3)
                nc.vector.tensor_tensor(bn_gdiff[:, at], bn_diff[:, at], vec[:, 1, k:k + 1], ALU.mult
                                        ).then_inc(bn_steps, 1)

            def scale_and_shift(j, vec, k):
                at = slice(j, j + 1)
                dve.wait_ge(bn_steps, 4 * j + 4)
                dve.wait_ge(bn_rstd, j + 1)
                nc.vector.tensor_tensor(bn_scale[:, at], bn_rs[:, at], vec[:, 1, k:k + 1], ALU.mult)
                nc.vector.scalar_tensor_tensor(bn_shift[:, at], bn_rs[:, at], bn_gdiff[:, at], vec[:, 2, k:k + 1],
                                               ALU.mult, ALU.add).then_inc(bn_ready, 1)

            def aggregate(n, u, first, last, job):
                if last >= 5 and not isinstance(n, int):
                    dve.wait_ge(y_ready, H1 * (n - 5) + H1)
                if first == 0:
                    dve.wait_ge(back_done, n + 1)
                    nc.vector.tensor_tensor(X[:, ds(n, 1), :], ps[:, 4:5, :], X[:, ds(n, 1), :],
                                            ALU.add).then_inc(x_added, 1)
                    dve.wait_ge(x_added, n + 1)
                if first <= 1 <= last:
                    variance(NT + n - 1)
                    hand_over(NT + n - 1)
                if first == 0:
                    halves(n)
                if job and u == 0:
                    hidden(job)
                if last >= 5:
                    t = n - 5
                    for k in range(H1):
                        if isinstance(n, int):
                            if (t, k) == (NT - 1, 1):
                                dve.wait_ge(lin_loaded, 64)
                                dve.wait_ge(y_stats, H1 * NT - 1)
                                batchnorm(0, st1[:, 0, :, :], vec1_sb, 0)
                            dve.wait_ge(y_ready, H1 * t + k + 1)
                        nc.vector.bn_stats(st1[:, k, ds(t, 1), :], y[:, k, ds(t, 1), :]).then_inc(y_stats, 1)
            closing_loop(cell, aggregate, dve, 6)
            scale_and_shift(0, vec1_sb, 0)
            dve.wait_ge(y_stats, H1 * NT)
            batchnorm(1, st1[:, 1, :, :], vec1_sb, 1)
            scale_and_shift(1, vec1_sb, 1)

            def copy_z(t, q):
                nc.vector.tensor_copy(z[:, ds(t, 1), :], ps[:, q:q + 1, :]).then_inc(z_ready, 1)

            def z_statistics(t, q):
                nc.vector.bn_stats(st2[:, ds(t, 1), :], ps[:, q:q + 1, :]).then_inc(z_stats, 1)

            with dve.Fori(0, NT // 2 - 1) as i:
                for q in range(2):
                    dve.wait_ge(lin2_done, 2 * i + q + 1)
                    copy_z(2 * i + q, q)
                    z_statistics(2 * i + q, q)
            dve.wait_ge(lin2_done, NT - 1)
            copy_z(NT - 2, 0)
            z_statistics(NT - 2, 0)
            dve.wait_ge(lin2_done, NT)
            z_statistics(NT - 1, 1)
            dve.wait_ge(z_stats, NT)
            batchnorm(H1, st2[:, :, :], vec2_sb, 0)
            scale_and_shift(H1, vec2_sb, 0)
            copy_z(NT - 1, 1)

            for t in range(4):
                dve.wait_ge(out_done, t + 1)
                nc.vector.tensor_tensor(X[:, t, :], ps[:, 2 + t, :], X[:, t, :], ALU.add).then_inc(out_ready, 1)

            def add_out(i, q):
                t = 4 * i + 2 * q
                dve.wait_ge(out_done, t + 2)
                nc.vector.tensor_tensor(X[:, ds(t, 2), :], ps[:, 2 + 2 * q:4 + 2 * q, :], X[:, ds(t, 2), :],
                                        ALU.add).then_inc(out_ready, 2)
            with dve.Fori(1, NT // 4) as i:
                add_out(i, 0)
                add_out(i, 1)

        @block.tensor
        def _(pe):
            adjT_mov = adj_sb[:, 1, :]

            pe.wait_ge(graph_loaded, 32)
            nc.tensor.matmul(ps[:, 7, 0:P], gcn_b_sb[:, 0, :], adjT_mov, start=True, stop=True).then_inc(row_bias_done, 1)

            def data_times(bank, data, moving, done):
                for b in range(TB):
                    m = nc.tensor.matmul(ps[:, bank, b * P:(b + 1) * P], data[:, b, :], moving, start=True, stop=True)
                m.then_inc(done, 1)

            def split_product(out_at, m, gt, hi, lo, start, stop):
                w = slice(gt * P, (gt + 1) * P)
                nc.tensor.matmul(out_at, w_hi[:, m, w], hi, start=start, stop=False)
                nc.tensor.matmul(out_at, w_hi[:, m, w], lo, start=False, stop=False)
                return nc.tensor.matmul(out_at, w_lo[:, m, w], hi, start=False, stop=stop)

            def convolutions(i, first, last):
                if last >= 4:
                    t = i - 4
                    if isinstance(i, int) and i == 4:
                        pe.wait_ge(w_ready, 1)
                    pe.wait_ge(h0_ready, t + 1)
                    at_least(pe, o_ready, t)
                    for k, gt in enumerate([I_, G_, O_]):
                        split_product(ps[:, 4 + k, :], 0, gt, h0_hi, h0_lo, True, True).then_inc(gate_done, 1)
                if first <= 3 <= last:
                    pe.wait_ge(u2_ready, i - 3 + 1)
                    data_times(3, u2, adjT_mov, conv2_done)
                if first <= 2 <= last:
                    pe.wait_ge(h1_ready, i - 2 + 1)
                    data_times(2, h1, gcn_w_sb[:, 1, :], u2_done)
                if first <= 1 <= last:
                    pe.wait_ge(agg_ready, i - 1 + 1)
                    nc.tensor.matmul(ps[:, 1, :], gcn_w_sb[:, 0, :], agg[:], start=True, stop=True
                                     ).then_inc(conv1_done, 1)
                if first == 0:
                    pe.wait_ge(f_ready, i + 1)
                    data_times(0, f_in, adjT_mov, agg_done)
                if isinstance(i, int) and i == 3:
                    pe.wait_ge(row_bias_ready, 1)
                    pe.wait_ge(ident_ready, 2)
                    pe.wait_ge(scaled_ready, 1)
                    nc.tensor.transpose(ps[:, 7, 0:P], norm[:, 0, :], ident[:]).then_inc(scaledT_done, 1)
            skewed_loop(pe, convolutions, 5)

            pe.wait_ge(ahatT_ready, 1)
            pe.wait_ge(w_ready, 7)
            def lstm_products(job):
                (p, s), g, q = STAGES[job.k], job.g, job.q
                n, m_ih = GB * windows(p), 2 * p - 3
                for gt in gate_order(s):
                    bank = ps[:, 4 * q + gt, 0:n]
                    a = split_product(bank, m_ih, gt, positions(h_hi, g, p, s), positions(h_lo, g, p, s),
                                      True, s == 0)
                    if s > 0:
                        a = split_product(bank, m_ih + 1, gt, rec_hi[:, ds(g, 1), 0:n],
                                          rec_lo[:, ds(g, 1), 0:n], False, True)
                    a.then_inc(gate_done, 1)

            def slot(job, prev, run):
                pe.wait_ge(hid_lo_ready, jobs_needed(job, *run))
                pe.wait_ge(o_ready, job.number - 1)
                lstm_products(job)
            lstm_slots(pe, slot)

            pe.wait_ge(lin_loaded, 64)

            def last_products(job):
                pe.wait_ge(hid_lo_ready, job.number - NG + 1)
                pe.wait_ge(o_ready, last_buffers(job))
                lstm_products(job)

            def aggregate(n, u, first, last, job):
                def first_linear(k):
                    t = n - 4
                    pe.wait_ge(agg_ready, NT + t + 1)
                    at_least(pe, y_ready, H1 * (t - 1) + k + 1)
                    nc.tensor.matmul(ps[:, 6 + k, :], lin1_sb[:, k * P:(k + 1) * P], agg2[u],
                                     start=True, stop=True).then_inc(lin1_done, 1)
                if last >= 4:
                    first_linear(0)
                if first == 0:
                    if isinstance(n, int) and n == 0:
                        pe.wait_ge(o_ready, LAST_START[0])
                    pe.wait_ge(hsum_ready, n + 1)
                    at_least(pe, x_added, n)
                    for b in range(TB):
                        m = nc.tensor.transpose(ps[:, 4, b * P:(b + 1) * P], hsum[u][:, b, :], ident[:])
                    m.then_inc(back_done, 1)
                if first <= 3 <= last:
                    pe.wait_ge(f_ready, NT + n - 3 + 1)
                    at_least(pe, agg_ready, NT + n - 3)
                    data_times(5, f_in, ahatT[:], agg_done)
                if last >= 4:
                    first_linear(1)
            closing_loop(last_products, aggregate, pe, 5)

            def second_linear(t, q):
                at_least(pe, z_stats, t - 1)
                for k in range(H1):
                    pe.wait_ge(yr_ready, H1 * t + k + 1)
                    m = nc.tensor.matmul(ps[:, q:q + 1, :], lin2_sb[:, k, :], y[:, k, ds(t, 1), :],
                                         start=(k == 0), stop=(k == H1 - 1))
                m.then_inc(lin2_done, 1)
            for t in range(4):
                second_linear(t, t % 2)
            with pe.Fori(1, NT // 4) as i:
                for t in range(4):
                    second_linear(4 * i + t, t % 2)

            def turn_out(t, h, n):
                pe.wait_ge(zt_ready, t + n)
                at_least(pe, out_ready, t + n - 4)
                for j in range(n * TB):
                    k, b = h + j // TB, j % TB
                    m = nc.tensor.transpose(ps[:, 2 + k, b * P:(b + 1) * P], zt[:, k, b * P:(b + 1) * P], ident[:])
                m.then_inc(out_done, n)
            for t in range(4):
                turn_out(t, t, 1)
            with pe.Fori(1, NT // 4) as i:
                turn_out(4 * i, 0, 2)
                turn_out(4 * i + 2, 2, 2)


def kernel(**inputs):
    import numpy as np
    import concourse.bacc as bacc
    from concourse.bass_utils import run_bass_kernel_spmd

    def a(name):
        return np.asarray(inputs[name])

    wih, whh = a("L0_gnn_Wih"), a("L0_gnn_Whh")
    order = [(wih, 0)] + [(w, p) for p in range(1, SKIPS) for w in (wih, whh)]
    arrays = {
        "x": a("x").transpose(1, 0, 2).reshape(P, NT, TC),
        "graph": np.stack([a("adj"), a("adj").T, a("L0_gnn_Wg0"), a("L0_gnn_Wg1")], 1),
        "gcn_b": np.stack([a("L0_gnn_bg0"), a("L0_gnn_bg1")], 0),
        "lstm_w": np.stack([w[p].T for w, p in order], 1),
        "lstm_b": np.stack([a(n).reshape(SKIPS * 4, P).T for n in ("L0_gnn_bih", "L0_gnn_bhh")], 1),
        "lin1_w": a("L1_gnn_W1").T,
        "lin2_w": a("L1_gnn_W2").T.reshape(H1, P, P).transpose(1, 0, 2),
        "vec1": np.stack([a(n).reshape(H1, P).T for n in ("L1_gnn_b1", "L1_gnn_g1", "L1_gnn_be1")], 1),
        "vec2": np.stack([a(n).reshape(1, P).T for n in ("L1_gnn_b2", "L1_gnn_g2", "L1_gnn_be2")], 1),
    }
    arrays = {k: np.ascontiguousarray(v) for k, v in arrays.items()}
    nc = bacc.Bacc("TRN2", target_bir_lowering=False, num_devices=1)
    args = [nc.dram_tensor(k, v.shape, mybir.dt.float32, kind="ExternalInput").ap() for k, v in arrays.items()]
    out = nc.dram_tensor("out", (P, NT, TC), mybir.dt.float32, kind="ExternalOutput").ap()
    gnn_kernel(nc, *args, out)
    r = run_bass_kernel_spmd(nc, [arrays], core_ids=[0]).results[0]["out"]
    return np.ascontiguousarray(r.reshape(P, NB, P).transpose(1, 0, 2))
```
